# Optimizing a Trainium2 kernel written in Bass

```python
import numpy as np
import jax
import jax.numpy as jnp

def _softmax(x, axis=-1):
    return jax.nn.softmax(x, axis=axis)

def _gelu(x):
    return jax.nn.gelu(x, approximate=True)

def _silu(x):
    return jax.nn.silu(x)

def _sigmoid(x):
    return jax.nn.sigmoid(x)

def _layernorm(x, axis=-1, eps=1e-05):
    m = jnp.mean(x, axis=axis, keepdims=True)
    v = jnp.var(x, axis=axis, keepdims=True)
    return (x - m) / jnp.sqrt(v + eps)

def _scatter_add(tgt, idx, src, axis=0):
    return tgt.at[idx].add(src)

def _segment_sum(src, seg, n):
    return jax.ops.segment_sum(src, seg, n)
kernel_name = 'mk_adaln_d1_jaxref_r8_395dfc'

def setup_inputs(seed: int=0):
    np.random.seed(seed)
    _w = jnp.asarray

    def _L0_attn_setup():
        import jax, jax.numpy as jnp
        import numpy as np
        HEADS = 16
        KV_HEADS = 4
        DIM_HEAD = 64
        SCALE = DIM_HEAD ** (-0.5)

        def _rotate_half(x):
            x1, x2 = jnp.split(x, 2, axis=-1)
            return jnp.concatenate((-x2, x1), axis=-1)

        def _rope_freqs(n, d):
            inv_freq = 1.0 / 10000.0 ** (jnp.arange(0, d, 2, dtype=jnp.float32) / d)
            freqs = jnp.einsum('i,j->ij', jnp.arange(n, dtype=jnp.float32), inv_freq)
            return jnp.concatenate((freqs, freqs), axis=-1)
        key = jax.random.key(seed)
        ks = jax.random.split(key, 4)
        b, n, dim = (2, 256, 128)
        inner = HEADS * DIM_HEAD
        s = dim ** (-0.5)
        return {'x': jax.random.normal(ks[0], (b, n, dim), jnp.float32), 'Wq': jax.random.normal(ks[1], (dim, inner), jnp.float32) * s, 'Wkv': jax.random.normal(ks[2], (dim, DIM_HEAD * KV_HEADS * 2), jnp.float32) * s, 'Wo': jax.random.normal(ks[3], (inner, dim), jnp.float32) * s, 'bo': jnp.zeros((dim,), jnp.float32)}
    _L0_attn_in = _L0_attn_setup()

    def _L0_ffn_setup():
        import jax, jax.numpy as jnp
        import numpy as np

        def _binarize(w):
            alpha = jax.lax.stop_gradient(jnp.mean(jnp.abs(w), axis=1, keepdims=True))
            bw = alpha * jnp.sign(w)
            return w + jax.lax.stop_gradient(bw - w)
        key = jax.random.key(seed)
        k1, k2, k3, k4, k5 = jax.random.split(key, 5)
        D, H = (128, 512)
        x = jax.random.normal(k1, (64, 196, D), dtype=jnp.float32)
        w1 = jax.random.normal(k2, (H, D), dtype=jnp.float32) * 0.02
        b1 = jax.random.normal(k3, (H,), dtype=jnp.float32) * 0.02
        w2 = jax.random.normal(k4, (D, H), dtype=jnp.float32) * 0.02
        b2 = jax.random.normal(k5, (D,), dtype=jnp.float32) * 0.02
        return {'x': x, 'w1': w1, 'b1': b1, 'w2': w2, 'b2': b2}
    _L0_ffn_in = _L0_ffn_setup()
    _L0_c = _w((lambda *s: np.random.randn(*s).astype(np.float32) * 0.05)(16, 128))
    _L0_wmod = _w((lambda *s: np.random.randn(*s).astype(np.float32) * 0.05)(128, 6 * 128) * 128 ** (-0.5))
    _d = {'L0_attn_x': _L0_attn_in['x'], 'L0_attn_Wq': _L0_attn_in['Wq'], 'L0_attn_Wkv': _L0_attn_in['Wkv'], 'L0_attn_Wo': _L0_attn_in['Wo'], 'L0_attn_bo': _L0_attn_in['bo'], 'L0_ffn_w1': _L0_ffn_in['w1'], 'L0_ffn_b1': _L0_ffn_in['b1'], 'L0_ffn_w2': _L0_ffn_in['w2'], 'L0_ffn_b2': _L0_ffn_in['b2'], 'L0_c': _L0_c, 'L0_wmod': _L0_wmod}
    _x0 = _d['L0_attn_x']
    _d['L0_attn_x'] = jax.random.normal(jax.random.fold_in(jax.random.key(seed), 1), (16, 256, 128), dtype=_x0.dtype)
    del _x0
    return _d

def reference(L0_attn_x, L0_attn_Wq, L0_attn_Wkv, L0_attn_Wo, L0_attn_bo, L0_ffn_w1, L0_ffn_b1, L0_ffn_w2, L0_ffn_b2, L0_c, L0_wmod):

    def _L0_attn_ref(x, Wq, Wkv, Wo, bo):
        import jax, jax.numpy as jnp
        import numpy as np
        HEADS = 16
        KV_HEADS = 4
        DIM_HEAD = 64
        SCALE = DIM_HEAD ** (-0.5)

        def _rotate_half(x):
            x1, x2 = jnp.split(x, 2, axis=-1)
            return jnp.concatenate((-x2, x1), axis=-1)

        def _rope_freqs(n, d):
            inv_freq = 1.0 / 10000.0 ** (jnp.arange(0, d, 2, dtype=jnp.float32) / d)
            freqs = jnp.einsum('i,j->ij', jnp.arange(n, dtype=jnp.float32), inv_freq)
            return jnp.concatenate((freqs, freqs), axis=-1)
        b, n, dim = x.shape
        g = HEADS // KV_HEADS
        q = (x @ Wq).reshape(b, n, HEADS, DIM_HEAD).transpose(0, 2, 1, 3)
        kv = (x @ Wkv).reshape(b, n, 2 * KV_HEADS, DIM_HEAD)
        k = kv[:, :, :KV_HEADS].transpose(0, 2, 1, 3)
        v = kv[:, :, KV_HEADS:].transpose(0, 2, 1, 3)
        freqs = _rope_freqs(n, DIM_HEAD)
        cos, sin = (jnp.cos(freqs), jnp.sin(freqs))
        q = q * cos + _rotate_half(q) * sin
        k = k * cos + _rotate_half(k) * sin
        k = jnp.repeat(k, g, axis=1)
        v = jnp.repeat(v, g, axis=1)
        dots = jnp.einsum('bhid,bhjd->bhij', q, k) * SCALE
        attn = jax.nn.softmax(dots, axis=-1)
        out = jnp.einsum('bhij,bhjd->bhid', attn, v)
        out = out.transpose(0, 2, 1, 3).reshape(b, n, HEADS * DIM_HEAD)
        return out @ Wo + bo

    def _L0_ffn_ref(x, w1, b1, w2, b2):
        import jax, jax.numpy as jnp
        import numpy as np

        def _binarize(w):
            alpha = jax.lax.stop_gradient(jnp.mean(jnp.abs(w), axis=1, keepdims=True))
            bw = alpha * jnp.sign(w)
            return w + jax.lax.stop_gradient(bw - w)
        bw1 = _binarize(w1)
        h = jnp.einsum('bsd,hd->bsh', x, bw1) + b1
        h = jax.nn.gelu(h, approximate=False)
        bw2 = _binarize(w2)
        out = jnp.einsum('bsh,dh->bsd', h, bw2) + b2
        return out
    x = L0_attn_x
    mod = (_silu(L0_c) @ L0_wmod).reshape(L0_c.shape[0], 6, 1, -1)
    sa, ca, ga, sb, cb, gb = (mod[:, 0], mod[:, 1], mod[:, 2], mod[:, 3], mod[:, 4], mod[:, 5])
    ga = (2 * (ga >= 0) - 1) * jnp.maximum(jnp.abs(ga), 0.25)
    gb = (2 * (gb >= 0) - 1) * jnp.maximum(jnp.abs(gb), 0.25)
    h = _layernorm(x, axis=-1) * (1 + ca) + sa
    x = x + ga * _L0_attn_ref(h, L0_attn_Wq, L0_attn_Wkv, L0_attn_Wo, L0_attn_bo)
    h = _layernorm(x, axis=-1) * (1 + cb) + sb
    x = x + gb * _L0_ffn_ref(h, L0_ffn_w1, L0_ffn_b1, L0_ffn_w2, L0_ffn_b2)
    return x

_drawn_inputs = setup_inputs


def setup_inputs(seed=0):
    import zlib

    import numpy as np

    out = dict(_drawn_inputs(seed))
    spreads = {'L0_attn_bo': (0.0, 0.325)}
    factors = {'L0_ffn_w1': 6.708, 'L0_ffn_b1': 8.0, 'L0_ffn_w2': 6.502, 'L0_ffn_b2': 8.0}
    for name, (base, spread) in spreads.items():
        noise = np.random.default_rng([zlib.crc32(name.encode()), seed]).standard_normal(out[name].shape)
        drawn = base * np.exp(spread * noise) if base else spread * noise
        out[name] = jnp.asarray(drawn.astype(out[name].dtype))
    for name, factor in factors.items():
        out[name] = (out[name] * factor).astype(out[name].dtype)
    return out
```

```python
from contextlib import ExitStack

import numpy as np

import concourse.bass as bass
from concourse import mybir

F32 = mybir.dt.float32
F32R = mybir.dt.float32r
ALU = mybir.AluOpType
ACT = mybir.ActivationFunctionType
AX = mybir.AxisListType

P = 128
B, N, D = 16, 256, 128
C = N // P
HEADS, KV, DH = 16, 4, 64
GROUP = HEADS // KV
INNER = HEADS * DH
PAIRS = HEADS // 2
QK = HEADS + KV
WIDE = (HEADS + 2 * KV) * DH
FF = 512
KF = FF // P
SCALE = DH ** -0.5
EPS = 1e-5

UNITS = [
    ([], [("xT", 0)]),
    ([("qkv", 0, 2)], [("qkv", 1, 2), ("qkv", 0, 0)]),
    ([("qkv", 1, 0), ("yT", 0)], [("qkv", 0, 1)]),
    ([("qkv", 1, 1), ("kt", 0), ("kt", 1)], [("qt", 0), ("qt", 1), ("zT", 0)]),
    ([("qt", 2), ("s", 0), ("s", 1)], [("qt", 3), ("s", 2), ("s", 3)]),
    ([("s", 4), ("s", 5), ("qt", 4)], [("s", 6), ("s", 7), ("mT", 0)]),
    ([("qt", 5), ("qt", 6), ("s", 8), ("s", 9)], [("qt", 7), ("s", 10), ("s", 11)]),
    ([("s", 12), ("s", 13)], [("s", 14), ("s", 15), ("mT", 1)]),
]
OUT_UNITS = ("yT", "zT")
PER_STEP = sum(len(a) + len(b) for a, b in UNITS)
QKV_ORDER = [(0, 2), (1, 2), (0, 0), (1, 0), (0, 1), (1, 1)]


class Step:

    def __init__(self, t, odd, **holds):
        self.t, self.odd, self.holds = t, odd, holds
        self.number = 2 * t + odd if isinstance(t, int) else None

    def __getattr__(self, name):
        return self.holds.get(name, False)

    def count(self, per, more, batch=0):
        return self.t * (2 * per) + (per * (self.odd + batch) + more)

    def batch(self, ahead):
        return self.t * 2 + (self.odd + ahead)

    def par(self, ahead):
        return (self.odd + ahead) % 2


def attention_steps(eng, body):
    body(Step(-1, 1, prep=True))
    body(Step(0, 0, attn=True, prep=True))
    with eng.Fori(0, (B - 2) // 2) as t:
        body(Step(t, 1, attn=True, prep=True, out=True))
        body(Step(t, 2, attn=True, prep=True, out=True))
    body(Step(B // 2 - 1, 1, attn=True, out=True))
    body(Step(B // 2, 0, out=True, tail=True))


def mlp_steps(eng, body):
    body(Step(-1, 1, norm=True))
    body(Step(0, 0, norm=True, ff1=True))
    body(Step(0, 1, norm=True, ff1=True, ff2=True))
    for odd in range(2):
        body(Step(1, odd, norm=True, ff1=True, ff2=True, store=True))
    with eng.Fori(2, B // 2 - 1) as t:
        for odd in range(2):
            body(Step(t, odd, norm=True, ff1=True, ff2=True, store=True))
    body(Step(B // 2 - 1, 0, norm=True, ff1=True, ff2=True, store=True))
    body(Step(B // 2 - 1, 1, ff1=True, ff2=True, store=True))
    body(Step(B // 2, 0, ff2=True, store=True))
    body(Step(B // 2, 1, store=True))


def units_of(st):
    return [(s, h, u) for s, halves in enumerate(UNITS) for h, units in enumerate(halves) for u in units
            if (st.out if u[0] in OUT_UNITS else st.prep)]


def first_unit(st):
    no_out = PER_STEP - len(OUT_UNITS)
    if st.number is not None and st.number <= 0:
        return 0, (st.number + 1) * no_out
    start = 2 * no_out - PER_STEP
    if st.tail:
        return 0, PER_STEP * (st.number - 1) + start + len(OUT_UNITS)
    return 2 * PER_STEP, PER_STEP * st.odd + start


def ring(st, slot, half):
    per_t, first = first_unit(st)
    return [(k, u, (first + k) % 2, st.t * (per_t // 2) + (first + k) // 2)
            for k, (s, h, u) in enumerate(units_of(st)) if (s, h) == (slot, half)]


def adaln_layer(nc, x, wq, wkv, wo, bo, w1, b1, w2, b2, c, wmod, cos, sin, out):
    ctx = ExitStack()
    with ctx:
        def sb(name, shape, dt=F32):
            return ctx.enter_context(nc.sbuf_tensor(name, shape, dt))

        def sem(name):
            return ctx.enter_context(nc.semaphore(name))

        ident = sb("ident", [P, P])
        minus_half = sb("minus_half", [P, C])
        xa = sb("xa", [P, B, C, D])
        w_all = sb("w_all", [P, WIDE])
        w_hi = sb("w_hi", [P, WIDE], F32R)
        w_lo = sb("w_lo", [P, WIDE], F32R)
        wo_sb = sb("wo_sb", [P, PAIRS, D])
        cos_sb = sb("cos_sb", [P, C, DH])
        sin_sb = sb("sin_sb", [P, C, DH])
        w1_sb = sb("w1_sb", [P, KF, D])
        w2_sb = sb("w2_sb", [P, FF])
        sign1 = sb("sign1", [P, KF, D])
        sign2 = sb("sign2", [P, FF])
        s1t = sb("s1t", [P, KF, P], F32R)
        s2t = sb("s2t", [P, KF, P])
        alpha1 = sb("alpha1", [P, KF])
        alpha2 = sb("alpha2", [P, 1])
        b1_sb = sb("b1_sb", [P, KF])
        b2_sb = sb("b2_sb", [P, 1])
        bo_sb = sb("bo_sb", [P, 1])
        c_sb = sb("c_sb", [B, D])
        c_exp = sb("c_exp", [B, D])
        c_silu = sb("c_silu", [B, D])
        c_t = sb("c_t", [P, B])
        wmod_sb = sb("wmod_sb", [P, 6 * D])
        mod = sb("mod", [P, 6, B])
        gate_sign = sb("gate_sign", [P, B])
        gate_abs = sb("gate_abs", [P, B])
        ga_bo = sb("ga_bo", [P, B])
        gb_alpha = sb("gb_alpha", [P, B])
        gb_b2 = sb("gb_b2", [P, B])

        stats = sb("stats", [P, C, 6])
        pause = sb("pause", [P, 1])
        mean_var = sb("mean_var", [P, C, 2])
        var_eps = sb("var_eps", [P, C])
        rstd = sb("rstd", [P, C])
        xn = sb("xn", [P, C, D])
        h_t = sb("h_t", [P, N])
        h_hi = sb("h_hi", [P, N], F32R)
        h_lo = sb("h_lo", [P, N], F32R)
        rot_a = [sb(f"rot_a{i}", [P, 8, DH]) for i in range(2)]
        rot_b = [sb(f"rot_b{i}", [P, 8, DH]) for i in range(2)]
        qk_rot = sb("qk_rot", [P, C, QK, 2, DH])
        v_sb = [sb(f"v{i}", [P, C, KV, DH + 1]) for i in range(2)]
        k_hi2 = [sb(f"k_hi2{i}", [P, KV, N], F32R) for i in range(2)]
        k_lo1 = [sb(f"k_lo1{i}", [DH + 1, KV, N], F32R) for i in range(2)]
        q_hilo = [sb(f"q_hilo{i}", [P, HEADS, N], F32R) for i in range(2)]
        q_him = [sb(f"q_him{i}", [DH + 1, HEADS, N], F32R) for i in range(2)]
        neg_max = sb("neg_max", [P, HEADS, C])
        neg_max_t = [sb(f"neg_max_t{i}", [HEADS, P], F32R) for i in range(2)]
        probs = [sb(f"probs{i}", [P, C, 2, N]) for i in range(2)]
        recip = [sb(f"recip{i}", [P, 4]) for i in range(2)]
        o_norm = [sb(f"o_norm{i}", [P, C, 2, DH]) for i in range(2)]
        o_t = [sb(f"o_t{i}", [P, PAIRS, N]) for i in range(2)]
        z_sb = sb("z_sb", [P, N])
        g_sb = [probs[i][:, :, :, :].rearrange("p c h i -> p (c h) i") for i in range(2)]
        y_sb = [sb(f"y{i}", [P, C, D]) for i in range(2)]

        st_ps = [ctx.enter_context(nc.psum_tensor(f"st_ps{i}", [P, C, 2 * N], F32)) for i in range(2)]
        o_ps = [ctx.enter_context(nc.psum_tensor(f"o_ps{i}", [P, 512], F32)) for i in range(2)]
        unit_ps = [ctx.enter_context(nc.psum_tensor(f"unit_ps{i}", [P, 512], F32)) for i in range(2)]

        x0_in, x_in, wq_in, wo_in, rope_in = sem("x0_in"), sem("x_in"), sem("wq_in"), sem("wo_in"), sem("rope_in")
        c_in, ffw_in, bias_in = sem("c_in"), sem("ffw_in"), sem("bias_in")
        consts_ready, ident_zero, ident_ready = sem("consts_ready"), sem("ident_zero"), sem("ident_ready")
        w_hi_ready, w_lo_ready = sem("w_hi_ready"), sem("w_lo_ready")
        silu_exp, silu_steps, silu_ready = sem("silu_exp"), sem("silu_steps"), sem("silu_ready")
        c_t_ps, c_t_ready, mod_ps, mod_raw, mod_steps = (
            sem("c_t_ps"), sem("c_t_ready"), sem("mod_ps"), sem("mod_raw"), sem("mod_steps"))
        signs_ready, sign_ps, signs_t_ready = sem("signs_ready"), sem("sign_ps"), sem("signs_t_ready")
        alpha_raw, alpha_ready = sem("alpha_raw"), sem("alpha_ready")

        unit_full = [sem(f"unit_full{i}") for i in range(2)]

        ln_stats, ln_aggr, ln_var, ln_rstd, ln_out = (
            sem("ln_stats"), sem("ln_aggr"), sem("ln_var"), sem("ln_rstd"), sem("ln_out"))
        h_ready, h_hi_ready, h_lo_ready = sem("h_ready"), sem("h_hi_ready"), sem("h_lo_ready")
        v_ready, rot_parts, rot_ready = sem("v_ready"), sem("rot_parts"), sem("rot_ready")
        k_hi_ready, k_lo_ready, q_hi_ready, q_lo_ready = (
            sem("k_hi_ready"), sem("k_lo_ready"), sem("q_hi_ready"), sem("q_lo_ready"))
        max_ready, max_t_ready = sem("max_ready"), sem("max_t_ready")
        max_in = [sem(f"max_in{i}") for i in range(2)]
        scores_full, probs_ready, pv_done = sem("scores_full"), sem("probs_ready"), sem("pv_done")
        recip_ready, norm_ready, ot_ps_full, ot_ready = sem("recip_ready"), sem("norm_ready"), sem("ot_ps_full"), sem("ot_ready")
        z_ready, x2_ready = sem("z_ready"), sem("x2_ready")
        mlp_xt_full, mlp_h_ready, mlp_h_hi_ready, mlp_h_lo_ready = (
            sem("mlp_xt_full"), sem("mlp_h_ready"), sem("mlp_h_hi_ready"), sem("mlp_h_lo_ready"))
        ff1_done, gelu_done, ff2_done, mlp_z_ready, mlp_zt_full, y_ready = (
            sem("ff1_done"), sem("gelu_done"), sem("ff2_done"), sem("mlp_z_ready"), sem("mlp_zt_full"), sem("y_ready"))
        y_out = [sem(f"y_out{i}") for i in range(2)]

        block = ctx.enter_context(nc.Block())

        @block.sync
        def _(sp):
            sp.dma_start(xa[:, 0, :, :], x[0].rearrange("(c p) d -> p c d", p=P)).then_inc(x0_in, 16)
            sp.dma_start(c_sb[:, :], c).then_inc(c_in, 16)
            sp.dma_start(wmod_sb[:, :], wmod).then_inc(c_in, 16)
            sp.dma_start(w_all[:, 0:INNER], wq).then_inc(wq_in, 16)
            sp.dma_start(w_all[:, INNER:WIDE], wkv).then_inc(wq_in, 16)
            sp.dma_start(cos_sb[:, :, :], cos.rearrange("(c p) d -> p c d", p=P)).then_inc(rope_in, 16)
            sp.dma_start(sin_sb[:, :, :], sin.rearrange("(c p) d -> p c d", p=P)).then_inc(rope_in, 16)
            sp.dma_start(bo_sb[:, :], bo.rearrange("(p o) -> p o", o=1)).then_inc(bias_in, 16)
            sp.dma_start(b2_sb[:, :], b2.rearrange("(p o) -> p o", o=1)).then_inc(bias_in, 16)
            for k in range(KF):
                sp.dma_start(b1_sb[:, k:k + 1], b1[k * P:(k + 1) * P].rearrange("(p o) -> p o", o=1)).then_inc(bias_in, 16)
            for b in range(1, B, 5):
                sp.dma_start(xa[:, b:b + 5, :, :], x[b:b + 5].rearrange("b (c p) d -> p b c d", p=P)).then_inc(x_in, 16)
            sp.dma_start(wo_sb[:, :, :], wo.rearrange("(s p) n -> p s n", p=P)).then_inc(wo_in, 16)
            sp.dma_start(w1_sb[:, :, :], w1.rearrange("(k p) d -> p k d", p=P)).then_inc(ffw_in, 16)
            sp.dma_start(w2_sb[:, :], w2).then_inc(ffw_in, 16)

            def step(st):
                if not st.prep:
                    return
                for half in range(2):
                    sp.wait_ge(max_t_ready, st.count(2, half + 1, 1))
                    sp.dma_start(q_him[st.par(1)][DH:DH + 1, half * 8:half * 8 + 8, :].bitcast(F32)
                                 .rearrange("o h (c i) -> o (h c) i", c=C),
                                 neg_max_t[half][:, :].bitcast(F32)).then_inc(max_in[half], 16)

            attention_steps(sp, step)

            with sp.Fori(0, B // 2) as t:
                for odd in range(2):
                    sp.wait_ge(y_ready, t * 2 + (odd + 1))
                    sp.dma_start(out[bass.ds(t * 2 + odd, 1)].rearrange("b (c p) d -> p (b c) d", p=P),
                                 y_sb[odd][:, :, :]).then_inc(y_out[odd], 16)
            for odd in range(2):
                sp.wait_ge(y_out[odd], 16 * (B // 2))

        @block.gpsimd
        def _(pool):
            pool.memset(ident[:, :], 0.0).then_inc(ident_zero, 1)
            pool.memset(minus_half[:, :], -0.5).then_inc(consts_ready, 1)
            pool.wait_ge(ident_zero, 1)
            pool.affine_select(out=ident[:, :], in_=ident[:, :], compare_op=ALU.not_equal, fill=1.0,
                               base=0, pattern=[[-1, P]], channel_multiplier=1).then_inc(ident_ready, 1)
            for i in range(2):
                pool.memset(v_sb[i][:, :, :, DH:DH + 1], 1.0).then_inc(consts_ready, 1)

            def rsqrt(done):
                pool.wait_ge(ln_var, done)
                pool.tensor_tensor(rstd[:, :], var_eps[:, :], minus_half[:, :], ALU.pow).then_inc(ln_rstd, 1)

            pool.wait_ge(consts_ready, 5)

            def step(st):
                if not st.prep:
                    return
                rsqrt(st.count(1, 1, 1))
                for k, (ch, n) in enumerate(QKV_ORDER):
                    heads = 4 if n == 2 else 8
                    pool.wait_ge(rot_parts, st.count(6, k + 1, 1))
                    twice = [P, heads, 2, DH]
                    pool.tensor_tensor(qk_rot[:, ch, 8 * n:8 * n + heads, :, :],
                                       rot_a[k % 2][:, 0:heads, :].unsqueeze(2).broadcast_to(twice),
                                       rot_b[k % 2][:, 0:heads, :].unsqueeze(2).broadcast_to(twice),
                                       ALU.add).then_inc(rot_ready, 1)

            attention_steps(pool, step)
            with pool.Fori(0, B // 2) as t:
                rsqrt(t * 2 + (B + 1))
                rsqrt(t * 2 + (B + 2))

        @block.scalar
        def _(act):
            act.wait_ge(c_in, 32)
            act.activation(c_exp[:, :], c_sb[:, :], ACT.Exp, scale=-1.0).then_inc(silu_exp, 1)
            act.wait_ge(wq_in, 32)
            act.activation(w_hi[:, :], w_all[:, :], ACT.Copy).then_inc(w_hi_ready, 1)
            act.wait_ge(c_t_ps, 1)
            act.activation(c_t[:, :], o_ps[0][:, 0:B], ACT.Copy).then_inc(c_t_ready, 1)
            act.wait_ge(mod_steps, 8)

            def unit(st, u, bank, before):
                kind, ps = u[0], unit_ps[bank]
                if kind in ("s", "zT") or (kind == "qkv" and u[2] != 2):
                    return
                act.wait_ge(unit_full[bank], before + 1)
                if kind == "xT":
                    b = st.batch(1)
                    act.activation(h_t[:, :], ps[:, 0:N], ACT.Identity, scale=mod[:, 1, bass.ds(b, 1)],
                                   bias=mod[:, 0, bass.ds(b, 1)]).then_inc(h_ready, 1)
                    act.wait_ge(h_ready, st.count(1, 1, 1))
                    act.activation(h_hi[:, :], h_t[:, :], ACT.Copy).then_inc(h_hi_ready, 1)
                if kind == "qkv":
                    act.activation(v_sb[st.par(1)][:, u[1], :, 0:DH],
                                   ps[:, 256:512].rearrange("p (g d) -> p g d", g=KV), ACT.Copy).then_inc(v_ready, 1)
                if kind == "kt":
                    g = 2 * u[1]
                    act.activation(k_hi2[st.par(1)][:, g:g + 2, :], ps[:, :].rearrange("p (g i) -> p g i", g=2),
                                   ACT.Copy).then_inc(k_hi_ready, 1)
                if kind == "qt":
                    h = 2 * u[1]
                    both = ps[:, :].rearrange("p (h i) -> p h i", h=2)
                    act.activation(q_hilo[st.par(1)][:, h:h + 2, :], both, ACT.Copy)
                    act.activation(q_him[st.par(1)][0:DH, h:h + 2, :], both[0:DH], ACT.Copy).then_inc(q_hi_ready, 1)
                if kind == "mT":
                    if st.number != -1:
                        act.wait_ge(max_in[u[1]], st.count(16, 0, 1))
                    act.activation(neg_max_t[u[1]][:, :], ps[0:HEADS, 0:P], ACT.Copy).then_inc(max_t_ready, 1)
                if kind == "yT":
                    b = st.batch(-1)
                    act.activation(z_sb[:, :], ps[:, 0:N], ACT.Identity, scale=mod[:, 2, bass.ds(b, 1)],
                                   bias=ga_bo[:, bass.ds(b, 1)]).then_inc(z_ready, 1)

            def step(st):
                for s in range(PAIRS):
                    if st.attn:
                        act.wait_ge(scores_full, st.count(8, s + 1))
                        act.activation(probs[s % 2][:, :, :, :].rearrange("p c h i -> p (c h i)"),
                                       st_ps[s % 2][:, :, :].rearrange("p c i -> p (c i)"),
                                       ACT.Exp, scale=SCALE).then_inc(probs_ready, 1)
                    for half in range(2):
                        for _, u, bank, before in ring(st, s, half):
                            unit(st, u, bank, before)
                    if (st.attn and s >= 2) or (st.out and s < 2):
                        pair, par = (s - 2) % 8, st.par(0 if s >= 2 else -1)
                        act.wait_ge(ot_ps_full, st.count(8, s - 1))
                        act.activation(o_t[par][:, pair, :], o_ps[s % 2][:, 0:N], ACT.Copy).then_inc(ot_ready, 1)

            attention_steps(act, step)

            act.wait_ge(ffw_in, 32)
            act.activation(sign1[:, :, :], w1_sb[:, :, :], ACT.Sign).then_inc(signs_ready, 1)
            act.activation(sign2[:, :], w2_sb[:, :], ACT.Sign).then_inc(signs_ready, 1)
            act.wait_ge(sign_ps, 1)
            act.activation(s1t[:, :, :], st_ps[0][:, 0, :].rearrange("p (k f) -> p k f", k=KF), ACT.Copy).then_inc(signs_t_ready, 1)
            act.activation(s2t[:, :, :], st_ps[0][:, 1, :].rearrange("p (k f) -> p k f", k=KF), ACT.Copy).then_inc(signs_t_ready, 1)
            act.wait_ge(alpha_ready, 1)

            def mlp_step(st):
                if st.norm:
                    b = st.batch(1)
                    act.wait_ge(mlp_xt_full, st.count(1, 1, 1))
                    if st.number != -1:
                        act.wait_ge(mlp_h_lo_ready, st.count(1, 0, 1))
                    act.activation(h_t[:, :], unit_ps[0][:, 0:N], ACT.Identity, scale=mod[:, 4, bass.ds(b, 1)],
                                   bias=mod[:, 3, bass.ds(b, 1)]).then_inc(mlp_h_ready, 1)
                    act.wait_ge(mlp_h_ready, st.count(1, 1, 1))
                    act.activation(h_hi[:, :], h_t[:, :], ACT.Copy).then_inc(mlp_h_hi_ready, 1)
                if st.ff2:
                    b = st.batch(-1)
                    act.wait_ge(ff2_done, st.count(1, 1, -1))
                    act.activation(z_sb[:, :], o_ps[st.par(-1)][:, 0:N], ACT.Identity,
                                   scale=gb_alpha[:, bass.ds(b, 1)],
                                   bias=gb_b2[:, bass.ds(b, 1)]).then_inc(mlp_z_ready, 1)

            def gelu(st):
                if st.ff1:
                    act.wait_ge(ff1_done, st.count(1, 1))
                    for k in range(KF):
                        act.activation(g_sb[st.par(0)][:, k, :], st_ps[st.par(0)][:, k // 2, (k % 2) * N:(k % 2) * N + N],
                                       ACT.Gelu, scale=alpha1[:, k:k + 1], bias=b1_sb[:, k:k + 1]).then_inc(gelu_done, 1)

            def both(st):
                gelu(st)
                mlp_step(st)

            mlp_steps(act, both)

        @block.vector
        def _(dve):
            def layer_norm(done, b):
                for ch in range(C):
                    ins = dve.bn_stats(stats[:, ch, :], xa[:, bass.ds(b, 1), ch, :].rearrange("p b d -> p (b d)"))
                ins.then_inc(ln_stats, 1)
                dve.wait_ge(ln_stats, done)
                dve.memset(pause[:, :], 0.0)
                for ch in range(C):
                    ins = dve.bn_aggr(mean_var[:, ch, :], stats[:, ch, :])
                ins.then_inc(ln_aggr, 1)
                dve.wait_ge(ln_aggr, done)
                dve.tensor_scalar(var_eps[:, :], mean_var[:, :, 1], EPS, None, ALU.add).then_inc(ln_var, 1)
                dve.wait_ge(ln_rstd, done)
                for ch in range(C):
                    ins = dve.tensor_scalar(xn[:, ch, :], xa[:, bass.ds(b, 1), ch, :].rearrange("p b d -> p (b d)"),
                                            mean_var[:, ch, 0:1], rstd[:, ch:ch + 1], ALU.subtract, ALU.mult)
                ins.then_inc(ln_out, 1)

            for i in range(2):
                dve.memset(k_lo1[i][DH:DH + 1, :, :].bitcast(F32), 1.0).then_inc(consts_ready, 1)
            dve.wait_ge(silu_exp, 1)
            dve.tensor_scalar(c_exp[:, :], c_exp[:, :], 1.0, None, ALU.add).then_inc(silu_steps, 1)
            dve.wait_ge(silu_steps, 1)
            dve.reciprocal(c_exp[:, :], c_exp[:, :]).then_inc(silu_steps, 1)
            dve.wait_ge(silu_steps, 2)
            dve.tensor_tensor(c_silu[:, :], c_sb[:, :], c_exp[:, :], ALU.mult).then_inc(silu_ready, 1)
            dve.wait_ge(w_hi_ready, 1)
            dve.tensor_tensor(w_lo[:, :], w_all[:, :], w_hi[:, :].bitcast(F32), ALU.subtract).then_inc(w_lo_ready, 1)
            dve.wait_ge(mod_ps, 1)
            dve.tensor_copy(mod[:, :, :], o_ps[1][:, 0:6 * B].rearrange("p (k b) -> p k b", k=6)).then_inc(mod_raw, 1)
            dve.wait_ge(mod_raw, 1)
            for k in (1, 4):
                dve.tensor_scalar(mod[:, k, :], mod[:, k, :], 1.0, None, ALU.add)
            dve.wait_ge(bias_in, 16 * (2 + KF))
            for n, k in enumerate((2, 5)):
                dve.tensor_scalar(gate_sign[:, :], mod[:, k, :], 0.0, 2.0, ALU.is_ge, ALU.mult)
                dve.scalar_tensor_tensor(gate_abs[:, :], mod[:, k, :], -1.0, mod[:, k, :], ALU.mult,
                                         ALU.max).then_inc(mod_steps, 1)
                dve.wait_ge(mod_steps, 4 * n + 1)
                dve.tensor_scalar(gate_abs[:, :], gate_abs[:, :], 0.25, None, ALU.max).then_inc(mod_steps, 1)
                dve.wait_ge(mod_steps, 4 * n + 2)
                dve.scalar_tensor_tensor(mod[:, k, :], gate_sign[:, :], -1.0, gate_abs[:, :], ALU.add,
                                         ALU.mult).then_inc(mod_steps, 1)
                dve.wait_ge(mod_steps, 4 * n + 3)
                bias, into = ((bo_sb, ga_bo), (b2_sb, gb_b2))[n]
                dve.tensor_scalar(into[:, :], mod[:, k, :], bias[:, 0:1], None, ALU.mult).then_inc(mod_steps, 1)

            def unit(st, u, bank, before):
                kind, ps = u[0], unit_ps[bank]
                if kind in ("mT", "yT"):
                    return
                dve.wait_ge(unit_full[bank], before + 1)
                if kind == "xT":
                    dve.wait_ge(h_hi_ready, st.count(1, 1, 1))
                    dve.tensor_tensor(h_lo[:, :], h_t[:, :], h_hi[:, :].bitcast(F32), ALU.subtract).then_inc(h_lo_ready, 1)
                if kind == "qkv":
                    ch, n = u[1:]
                    k, heads = QKV_ORDER.index((ch, n)), 4 if n == 2 else 8
                    if n == 2:
                        dve.wait_ge(v_ready, st.count(2, ch + 1, 1))
                    if st.number != -1 or k >= 2:
                        dve.wait_ge(rot_ready, st.count(6, k - 1, 1))
                    raw = ps[:, 0:heads * DH].rearrange("p (h d) -> p h d", h=heads)
                    halves = ps[:, 0:heads * DH].rearrange("p (h t d) -> p h t d", h=heads, t=2)
                    dve.tensor_tensor(rot_a[k % 2][:, 0:heads, :], raw,
                                      cos_sb[:, ch:ch + 1, :].broadcast_to([P, heads, DH]), ALU.mult)
                    dve.tensor_tensor(rot_b[k % 2][:, 0:heads, :].rearrange("p h (t d) -> p h t d", t=2),
                                      halves[:, :, ::-1, :],
                                      sin_sb[:, ch:ch + 1, :].broadcast_to([P, heads, DH])
                                      .rearrange("p h (t d) -> p h t d", t=2), ALU.mult).then_inc(rot_parts, 1)
                if kind == "kt":
                    g = 2 * u[1]
                    dve.wait_ge(k_hi_ready, st.count(2, u[1] + 1, 1))
                    dve.tensor_tensor(k_lo1[st.par(1)][0:DH, g:g + 2, :],
                                      ps[0:DH, :].rearrange("p (g i) -> p g i", g=2),
                                      k_hi2[st.par(1)][0:DH, g:g + 2, :].bitcast(F32),
                                      ALU.subtract).then_inc(k_lo_ready, 1)
                if kind == "qt":
                    h = 2 * u[1]
                    low = q_hilo[st.par(1)][DH:P, h:h + 2, :]
                    dve.wait_ge(q_hi_ready, st.count(8, u[1] + 1, 1))
                    dve.tensor_tensor(low, ps[DH:P, :].rearrange("p (h i) -> p h i", h=2), low.bitcast(F32),
                                      ALU.subtract).then_inc(q_lo_ready, 1)
                if kind == "s":
                    dve.tensor_reduce(neg_max[:, u[1], :], ps[:, :].rearrange("p (c j) -> p c j", c=C), AX.X, ALU.max,
                                      negate=True).then_inc(max_ready, 1)
                if kind == "zT":
                    b = st.batch(-1)
                    dve.tensor_tensor(xa[:, bass.ds(b, 1), :, :].rearrange("p b c d -> p (b c) d"),
                                      ps[:, 0:N].rearrange("p (c d) -> p c d", c=C),
                                      xa[:, bass.ds(b, 1), :, :].rearrange("p b c d -> p (b c) d"),
                                      ALU.add).then_inc(x2_ready, 1)

            def step(st):
                for s in range(PAIRS):
                    if s == 0 and st.prep:
                        if st.number == -1:
                            dve.wait_ge(x0_in, 16)
                        layer_norm(st.count(1, 1, 1), st.batch(1))
                    for _, u, bank, before in ring(st, s, 0):
                        unit(st, u, bank, before)
                    if (st.attn and s >= 1) or (st.out and s < 1):
                        i = (s - 1) % 2
                        groups = o_ps[i][:, 0:4 * (DH + 1)].rearrange("p (k e) -> p k e", e=DH + 1)
                        dve.wait_ge(pv_done, st.count(8, s))
                        dve.reciprocal(recip[i][:, :].unsqueeze(2), groups[:, :, DH:DH + 1]).then_inc(recip_ready, 1)
                        dve.wait_ge(recip_ready, st.count(8, s))
                        dve.tensor_tensor(o_norm[i][:, :, :, :].rearrange("p c h d -> p h c d"),
                                          groups[:, :, 0:DH].rearrange("p (h c) d -> p h c d", h=2),
                                          recip[i][:, :].rearrange("p (h c) -> p h c", h=2).unsqueeze(3)
                                          .broadcast_to([P, 2, C, DH]), ALU.mult).then_inc(norm_ready, 1)
                    for _, u, bank, before in ring(st, s, 1):
                        unit(st, u, bank, before)
                if st.number == -1:
                    dve.wait_ge(x_in, 48)

            dve.wait_ge(rope_in, 32)
            attention_steps(dve, step)

            dve.wait_ge(ffw_in, 32)
            dve.tensor_reduce(alpha1[:, :], w1_sb[:, :, :], AX.X, ALU.add, apply_absolute_value=True)
            dve.tensor_reduce(alpha2[:, :], w2_sb[:, :], AX.X, ALU.add, apply_absolute_value=True).then_inc(alpha_raw, 1)
            dve.wait_ge(alpha_raw, 1)
            dve.tensor_scalar(alpha1[:, :], alpha1[:, :], 1.0 / D, None, ALU.mult)
            dve.tensor_scalar(gb_alpha[:, :], mod[:, 5, :], alpha2[:, 0:1], 1.0 / FF, ALU.mult, ALU.mult).then_inc(alpha_ready, 1)

            def mlp_step(st):
                if st.norm:
                    layer_norm(st.count(1, B + 1, 1), st.batch(1))
                    dve.wait_ge(mlp_h_hi_ready, st.count(1, 1, 1))
                    if st.number != -1:
                        dve.wait_ge(ff1_done, st.count(1, 1))
                    dve.tensor_tensor(h_lo[:, :], h_t[:, :], h_hi[:, :].bitcast(F32), ALU.subtract).then_inc(mlp_h_lo_ready, 1)
                if st.store:
                    b, par = st.batch(-2), st.par(0)
                    dve.wait_ge(mlp_zt_full, st.count(1, 1, -2))
                    if st.number not in (2, 3):
                        dve.wait_ge(y_out[par], st.t * 16 + -16)
                    dve.tensor_tensor(y_sb[par][:, :, :], unit_ps[1][:, 0:N].rearrange("p (c d) -> p c d", c=C),
                                      xa[:, bass.ds(b, 1), :, :].rearrange("p b c d -> p (b c) d"),
                                      ALU.add).then_inc(y_ready, 1)

            mlp_steps(dve, mlp_step)

        @block.tensor
        def _(pe):
            pe.wait_ge(ident_ready, 1)
            pe.wait_ge(silu_ready, 1)
            pe.transpose(o_ps[0][:, 0:B], c_silu[:, :], ident[0:B, 0:B]).then_inc(c_t_ps, 1)
            pe.wait_ge(c_t_ready, 1)
            for k in range(6):
                ins = pe.matmul(o_ps[1][:, k * B:(k + 1) * B], wmod_sb[:, k * D:(k + 1) * D], c_t[:, :], start=True, stop=True)
            ins.then_inc(mod_ps, 1)

            def released_by(st, u, back):
                kind, ahead, behind = u[0], 1 - back, -1 - back
                return {
                    "xT": lambda: (h_ready, st.count(1, 1, ahead)),
                    "qkv": lambda: (rot_parts, st.count(6, QKV_ORDER.index(u[1:]) + 1, ahead)),
                    "kt": lambda: (k_lo_ready, st.count(2, u[1] + 1, ahead)),
                    "qt": lambda: (q_lo_ready, st.count(8, u[1] + 1, ahead)),
                    "s": lambda: (max_ready, st.count(16, u[1] + 1, ahead)),
                    "mT": lambda: (max_t_ready, st.count(2, u[1] + 1, ahead)),
                    "yT": lambda: (z_ready, st.count(1, 1, behind)),
                    "zT": lambda: (x2_ready, st.count(1, 1, behind)),
                }[kind]()

            def unit(st, place, u, bank):
                kind, ps, par = u[0], unit_ps[bank], st.par(1)
                mine = [x[2] for x in units_of(st)]
                if place >= 2:
                    pe.wait_ge(*released_by(st, mine[place - 2], 0))
                elif st.number != -1:
                    before = [x[2] for x in units_of(Step(0, 0, prep=not st.tail, out=st.number not in (0, 1)))]
                    pe.wait_ge(*released_by(st, before[place - 2], 1))
                if kind == "xT":
                    pe.wait_ge(ln_out, st.count(1, 1, 1))
                    for ch in range(C):
                        ins = pe.transpose(ps[:, ch * P:(ch + 1) * P], xn[:, ch, :], ident[:, :])
                if kind == "qkv":
                    ch, n = u[1:]
                    if (ch, n) == QKV_ORDER[0]:
                        pe.wait_ge(h_lo_ready, st.count(1, 1, 1))
                        if st.number == -1:
                            pe.wait_ge(w_lo_ready, 1)
                    own, cols = slice(ch * P, (ch + 1) * P), slice(n * 512, (n + 1) * 512)
                    pe.matmul(ps[:, :], h_hi[:, own], w_hi[:, cols], start=True, stop=False)
                    pe.matmul(ps[:, :], h_hi[:, own], w_lo[:, cols], start=False, stop=False)
                    ins = pe.matmul(ps[:, :], h_lo[:, own], w_hi[:, cols], start=False, stop=True)
                if kind in ("kt", "qt"):
                    first = 2 * u[1] + (HEADS if kind == "kt" else 0)
                    if u[1] == 0:
                        pe.wait_ge(rot_ready, st.count(6, 2 if kind == "kt" else 4, 1))
                    if kind == "qt" and u[1] == 4:
                        pe.wait_ge(rot_ready, st.count(6, 6, 1))
                    for h in range(2):
                        for ch in range(C):
                            ins = pe.transpose(ps[:, h * N + ch * P:h * N + (ch + 1) * P],
                                               qk_rot[:, ch, first + h, :, :].rearrange("p t d -> p (t d)"),
                                               ident[:, :])
                if kind == "s":
                    h, g = u[1], u[1] // GROUP
                    if h % 2 == 0:
                        pe.wait_ge(q_hi_ready, st.count(8, h // 2 + 1, 1))
                    if h % 8 == 0:
                        pe.wait_ge(k_hi_ready, st.count(2, h // 8 + 1, 1))
                    for ch in range(C):
                        ins = pe.matmul(ps[:, ch * N:(ch + 1) * N], q_him[par][0:DH, h, ch * P:(ch + 1) * P],
                                        k_hi2[par][0:DH, g, :], start=True, stop=True)
                if kind == "mT":
                    pe.wait_ge(max_ready, st.count(16, 8 * (u[1] + 1), 1))
                    ins = pe.transpose(ps[0:HEADS, 0:P], neg_max[:, 8 * u[1]:8 * u[1] + 8, :].rearrange("p h c -> p (h c)"),
                                       ident[:, :])
                if kind == "yT":
                    pe.wait_ge(ot_ready, st.count(8, 0))
                    for s in range(PAIRS):
                        ins = pe.matmul(ps[:, 0:N], wo_sb[:, s, :], o_t[st.par(-1)][:, s, :], start=s == 0, stop=s == PAIRS - 1)
                if kind == "zT":
                    pe.wait_ge(z_ready, st.count(1, 1, -1))
                    for ch in range(C):
                        ins = pe.transpose(ps[:, ch * P:(ch + 1) * P], z_sb[:, ch * P:(ch + 1) * P], ident[:, :])
                ins.then_inc(unit_full[bank], 1)

            def step(st):
                if st.number == 0:
                    pe.wait_ge(consts_ready, 5)
                    pe.wait_ge(wo_in, 16)
                for s in range(PAIRS):
                    if st.attn:
                        par, g = st.par(0), 2 * s // GROUP
                        if s % 4 == 0:
                            pe.wait_ge(k_lo_ready, st.count(2, s // 4 + 1))
                            pe.wait_ge(max_in[s // 4], st.count(16, 16))
                        pe.wait_ge(q_lo_ready, st.count(8, s + 1))
                        if st.number != 0 or s >= 2:
                            pe.wait_ge(probs_ready, st.count(8, s - 1))
                        for jc in range(C):
                            js = slice(jc * P, (jc + 1) * P)
                            pe.matmul(st_ps[s % 2][:, jc, :], k_hi2[par][:, g, js],
                                      q_hilo[par][:, 2 * s:2 * s + 2, :].rearrange("p h i -> p (h i)"), start=True, stop=False)
                            ins = pe.matmul(st_ps[s % 2][:, jc, :], k_lo1[par][:, g, js],
                                            q_him[par][:, 2 * s:2 * s + 2, :].rearrange("p h i -> p (h i)"),
                                            start=False, stop=True)
                        ins.then_inc(scores_full, 1)
                    for place, u, bank, _ in ring(st, s, 0):
                        unit(st, place, u, bank)
                    if (st.attn and s >= 1) or (st.out and s < 1):
                        pair, par = (s - 1) % 8, st.par(0 if s >= 1 else -1)
                        i, g = pair % 2, 2 * pair // GROUP
                        pe.wait_ge(probs_ready, st.count(8, s))
                        if st.number != 0 or s >= 3:
                            pe.wait_ge(ot_ready, st.count(8, s - 2))
                        for h in range(2):
                            for ch in range(C):
                                k = (h * C + ch) * (DH + 1)
                                for jc in range(C):
                                    ins = pe.matmul(o_ps[i][:, k:k + DH + 1], probs[i][:, jc, h, ch * P:(ch + 1) * P],
                                                    v_sb[par][:, jc, g, :], start=jc == 0, stop=jc == C - 1)
                        ins.then_inc(pv_done, 1)
                    for place, u, bank, _ in ring(st, s, 1):
                        unit(st, place, u, bank)
                    if (st.attn and s >= 2) or (st.out and s < 2):
                        i = s % 2
                        pe.wait_ge(norm_ready, st.count(8, s - 1))
                        for ch in range(C):
                            ins = pe.transpose(o_ps[i][:, ch * P:(ch + 1) * P],
                                               o_norm[i][:, ch, :, :].rearrange("p h d -> p (h d)"), ident[:, :])
                        ins.then_inc(ot_ps_full, 1)

            attention_steps(pe, step)

            def mlp_step(st):
                if st.store:
                    pe.wait_ge(mlp_z_ready, st.count(1, 1, -2))
                    if st.number != 2:
                        pe.wait_ge(y_ready, st.count(1, 0, -2))
                    for ch in range(C):
                        ins = pe.transpose(unit_ps[1][:, ch * P:(ch + 1) * P], z_sb[:, ch * P:(ch + 1) * P], ident[:, :])
                    ins.then_inc(mlp_zt_full, 1)
                if st.ff1:
                    pe.wait_ge(mlp_h_lo_ready, st.count(1, 1))
                    if st.number not in (0, 1):
                        pe.wait_ge(gelu_done, st.count(KF, 0, -1))
                    for k in range(KF):
                        into = st_ps[st.par(0)][:, k // 2, (k % 2) * N:(k % 2) * N + N]
                        pe.matmul(into, s1t[:, k, :], h_hi[:, :], start=True, stop=False)
                        ins = pe.matmul(into, s1t[:, k, :], h_lo[:, :], start=False, stop=True)
                    ins.then_inc(ff1_done, 1)
                if st.norm:
                    pe.wait_ge(ln_out, st.count(1, B + 1, 1))
                    if st.number != -1:
                        pe.wait_ge(mlp_h_ready, st.count(1, 0, 1))
                    for ch in range(C):
                        ins = pe.transpose(unit_ps[0][:, ch * P:(ch + 1) * P], xn[:, ch, :], ident[:, :])
                    ins.then_inc(mlp_xt_full, 1)
                if st.ff2:
                    pe.wait_ge(gelu_done, st.count(KF, 0))
                    if st.number not in (1, 2):
                        pe.wait_ge(mlp_z_ready, st.count(1, 0, -2))
                    for k in range(KF):
                        ins = pe.matmul(o_ps[st.par(-1)][:, 0:N], s2t[:, k, :], g_sb[st.par(-1)][:, k, :],
                                        start=k == 0, stop=k == KF - 1)
                    ins.then_inc(ff2_done, 1)

            pe.wait_ge(signs_ready, 2)
            pe.wait_ge(probs_ready, B * PAIRS)
            pe.wait_ge(ot_ready, B * PAIRS)
            pe.wait_ge(z_ready, B)
            pe.wait_ge(x2_ready, B)
            for k in range(KF):
                pe.transpose(st_ps[0][:, 0, k * P:(k + 1) * P], sign1[:, k, :], ident[:, :])
            for k in range(KF):
                ins = pe.transpose(st_ps[0][:, 1, k * P:(k + 1) * P], sign2[:, k * P:(k + 1) * P], ident[:, :])
            ins.then_inc(sign_ps, 1)
            pe.wait_ge(signs_t_ready, 2)
            mlp_steps(pe, mlp_step)


_ORDER = ["L0_attn_x", "L0_attn_Wq", "L0_attn_Wkv", "L0_attn_Wo", "L0_attn_bo", "L0_ffn_w1", "L0_ffn_b1",
          "L0_ffn_w2", "L0_ffn_b2", "L0_c", "L0_wmod"]


def rotary_tables():
    inv_freq = (1.0 / 10000.0 ** (np.arange(0, DH, 2, dtype=np.float32) / np.float32(DH))).astype(np.float32)
    freqs = np.arange(N, dtype=np.float32)[:, None] * inv_freq[None, :]
    cos, sin = np.cos(freqs), np.sin(freqs)
    return (np.concatenate([cos, cos], 1).astype(np.float32), np.concatenate([-sin, sin], 1).astype(np.float32))


def kernel(**inputs):
    import concourse.bacc as bacc
    from concourse.bass_utils import run_bass_kernel_spmd

    nc = bacc.Bacc("TRN2", target_bir_lowering=False, num_devices=1)
    cos, sin = rotary_tables()
    arrays = {f"in_{name}": np.ascontiguousarray(inputs[name]) for name in _ORDER}
    arrays["in_cos"], arrays["in_sin"] = cos, sin
    args = [nc.dram_tensor(name, a.shape, F32, kind="ExternalInput").ap() for name, a in arrays.items()]
    out = nc.dram_tensor("out_x", (B, N, D), F32, kind="ExternalOutput").ap()
    adaln_layer(nc, *args, out)
    r = run_bass_kernel_spmd(nc, [arrays], core_ids=[0])
    return r.results[0]["out_x"]
```

```python
from contextlib import ExitStack

import numpy as np

import concourse.bass as bass
from concourse import mybir

F32 = mybir.dt.float32
F32R = mybir.dt.float32r
ALU = mybir.AluOpType
ACT = mybir.ActivationFunctionType
AX = mybir.AxisListType

P = 128
B, N, D = 16, 256, 128
C = N // P
HEADS, KV, DH = 16, 4, 64
GROUP = HEADS // KV
INNER = HEADS * DH
PAIRS = HEADS // 2
QK = HEADS + KV
WIDE = (HEADS + 2 * KV) * DH
FF = 512
KF = FF // P
SCALE = DH ** -0.5
EPS = 1e-5

UNITS = [
    [("xT", 0)],
    [("qkv", 0, 2), ("qkv", 1, 2), ("qkv", 0, 0)],
    [("qkv", 1, 0), ("yT", 0), ("qkv", 0, 1)],
    [("qkv", 1, 1), ("kt", 0), ("kt", 1), ("qt", 0), ("zT", 0)],
    [("qt", 1), ("s", 0), ("s", 1), ("qt", 2), ("s", 2), ("s", 3)],
    [("qt", 3), ("s", 4), ("s", 5), ("qt", 4), ("s", 6), ("s", 7)],
    [("mT", 0), ("qt", 5), ("s", 8), ("s", 9), ("qt", 6), ("s", 10), ("s", 11)],
    [("qt", 7), ("s", 12), ("s", 13), ("s", 14), ("s", 15), ("mT", 1)],
]
ALL_UNITS = [(slot, u) for slot, units in enumerate(UNITS) for u in units]
OUT_UNITS = ("yT", "zT")
QKV_ORDER = [(0, 2), (1, 2), (0, 0), (1, 0), (0, 1), (1, 1)]
UNIT_BANK = [k % 3 for k in range(len(ALL_UNITS) - 1)] + [1]
SCORE_BANK = [k % 3 for k in range(2 * PAIRS - 1)] + [1]
WORK = [("norm",), ("scores", 0), ("scores", 1), ("pv", 0), ("pv", 1), ("ot",), ("pv", 2), ("pv", 3)]


class Step:

    def __init__(self, t, odd, **holds):
        self.t, self.odd, self.holds = t, odd, holds
        self.number = 2 * t + odd if isinstance(t, int) else None

    def __getattr__(self, name):
        return self.holds.get(name, False)

    def count(self, per, more, batch=0):
        return self.t * (2 * per) + (per * (self.odd + batch) + more)

    def batch(self, ahead):
        return self.t * 2 + (self.odd + ahead)

    def par(self, ahead):
        return (self.odd + ahead) % 2


def attention_steps(eng, body):
    body(Step(-1, 1, prep=True))
    body(Step(0, 0, attn=True, prep=True))
    with eng.Fori(0, (B - 2) // 2) as t:
        body(Step(t, 1, attn=True, prep=True, out=True))
        body(Step(t, 2, attn=True, prep=True, out=True))
    body(Step(B // 2 - 1, 1, attn=True, out=True))
    body(Step(B // 2, 0, out=True, tail=True))


def mlp_steps(eng, body):
    def mlp_step(t, odd):
        n = 2 * t + odd
        body(Step(t, odd, norm=n < B - 2, mod=-1 <= n < B - 1, ff1=0 <= n < B, ff2=1 <= n <= B, store=n >= 2))

    for n in range(-2, 4):
        mlp_step(n // 2, n % 2)
    with eng.Fori(2, B // 2 - 1) as t:
        for odd in range(2):
            body(Step(t, odd, norm=True, mod=True, ff1=True, ff2=True, store=True))
    for n in range(B - 2, B + 2):
        mlp_step(n // 2, n % 2)


def has(st, u):
    return st.out if u[0] in OUT_UNITS else st.prep


def units(st, slot):
    return [(k, u) for k, (s, u) in enumerate(ALL_UNITS) if s == slot and has(st, u)]


def slot_order(st, s):
    held = {"scores": st.attn, "pv": st.attn if s >= 1 else st.out,
            "norm": st.attn if s >= 2 else st.out, "ot": st.attn if s >= 2 else st.out}
    rest, order = units(st, s), []
    for w in WORK:
        if held[w[0]]:
            order.append((None, w))
            if rest and w[0] in ("scores", "pv"):
                order.append(rest.pop(0))
    return order + rest


def nth_unit(st, place):
    mine = sum(has(st, u) for _, u in ALL_UNITS[:place + 1])
    every, few = len(ALL_UNITS), len(ALL_UNITS) - len(OUT_UNITS)
    if st.number is not None and st.number <= 0:
        return (st.number + 1) * few + mine
    if st.tail:
        return 2 * few + (B - 2) * every + len(OUT_UNITS) + mine
    return st.count(every, 2 * few - every + mine)


def last_in_bank(st, place):
    for k in range(place - 1, -1, -1):
        if UNIT_BANK[k] == UNIT_BANK[place] and has(st, ALL_UNITS[k][1]):
            return ALL_UNITS[k][1], 0
    if st.number == -1:
        return None
    before = Step(0, 0, prep=not st.tail, out=st.number not in (0, 1))
    for k in range(len(ALL_UNITS) - 1, -1, -1):
        if UNIT_BANK[k] == UNIT_BANK[place] and has(before, ALL_UNITS[k][1]):
            return ALL_UNITS[k][1], 1
    return None


def adaln_layer(nc, x, wq, wkv, wo, bo, w1, b1, w2, b2, c, wmod, cos, sin, out):
    ctx = ExitStack()
    with ctx:
        def sb(name, shape, dt=F32):
            return ctx.enter_context(nc.sbuf_tensor(name, shape, dt))

        def sem(name):
            return ctx.enter_context(nc.semaphore(name))

        ident = sb("ident", [P, P])
        ident_r = sb("ident_r", [P, P], F32R)
        minus_half = sb("minus_half", [P, C])
        xa = sb("xa", [P, B, C, D])
        w_all = sb("w_all", [P, WIDE])
        w_hi = sb("w_hi", [P, WIDE], F32R)
        w_lo = sb("w_lo", [P, WIDE], F32R)
        wo_sb = sb("wo_sb", [P, PAIRS, D])
        cos_sb = sb("cos_sb", [P, C, DH])
        sin_sb = sb("sin_sb", [P, C, DH])
        w1_sb = sb("w1_sb", [P, KF, D])
        w2_sb = sb("w2_sb", [P, FF])
        sign1 = sb("sign1", [P, KF, D])
        sign2 = sb("sign2", [P, FF])
        s1t = sb("s1t", [P, KF, P], F32R)
        s2t = sb("s2t", [P, KF, P])
        alpha1 = sb("alpha1", [P, KF])
        alpha2 = sb("alpha2", [P, 1])
        b1_sb = sb("b1_sb", [P, KF])
        b2_sb = sb("b2_sb", [P, 1])
        bo_sb = sb("bo_sb", [P, 1])
        c_sb = sb("c_sb", [B, D])
        c_exp = sb("c_exp", [B, D])
        c_silu = sb("c_silu", [B, D])
        c_t = sb("c_t", [P, B])
        wmod_sb = sb("wmod_sb", [P, 6 * D])
        mod = sb("mod", [P, 6, B])
        gate_sign = sb("gate_sign", [P, B])
        gate_abs = sb("gate_abs", [P, B])
        ga_bo = sb("ga_bo", [P, B])
        gb_alpha = sb("gb_alpha", [P, B])
        gb_b2 = sb("gb_b2", [P, B])

        stats = sb("stats", [P, C, 6])
        pause = sb("pause", [P, 1])
        mean_var = sb("mean_var", [P, C, 2])
        var_eps = sb("var_eps", [P, C])
        rstd = sb("rstd", [P, C])
        xn = sb("xn", [P, C, D])
        h_t = sb("h_t", [P, N])
        h_hi = [sb(f"h_hi{i}", [P, N], F32R) for i in range(2)]
        h_lo = [sb(f"h_lo{i}", [P, N], F32R) for i in range(2)]
        rot_a = [sb(f"rot_a{i}", [P, 8, DH]) for i in range(2)]
        rot_b = [sb(f"rot_b{i}", [P, 8, DH]) for i in range(2)]
        rot_sum = sb("rot_sum", [P, 8, DH])
        qk_rot = sb("qk_rot", [P, C, QK, 2, DH], F32R)
        v_sb = [sb(f"v{i}", [P, C, KV, DH + 1]) for i in range(2)]
        k_hi2 = [sb(f"k_hi2{i}", [P, KV, N], F32R) for i in range(2)]
        k_lo1 = [sb(f"k_lo1{i}", [DH + 1, KV, N], F32R) for i in range(2)]
        q_hilo = [sb(f"q_hilo{i}", [P, HEADS, N], F32R) for i in range(2)]
        q_him = [sb(f"q_him{i}", [DH + 1, HEADS, N], F32R) for i in range(2)]
        neg_max = sb("neg_max", [P, HEADS, C])
        neg_max_t = [sb(f"neg_max_t{i}", [HEADS, P], F32R) for i in range(2)]
        probs = [sb(f"probs{i}", [P, C, 2, N]) for i in range(2)]
        recip = [sb(f"recip{i}", [P, 4]) for i in range(2)]
        o_norm = [sb(f"o_norm{i}", [P, C, 2, DH]) for i in range(2)]
        o_t = [sb(f"o_t{i}", [P, PAIRS, N]) for i in range(2)]
        z_sb = sb("z_sb", [P, N])
        g_sb = [probs[i][:, :, :, :].rearrange("p c h i -> p (c h) i") for i in range(2)]
        y_sb = [w_all[:, i * C * D:(i + 1) * C * D].rearrange("p (c d) -> p c d", c=C) for i in range(2)]

        def banks(name, n):
            return [ctx.enter_context(nc.psum_tensor(f"{name}{i}", [P, 512], F32)) for i in range(n)]

        score_ps, o_ps, unit_ps = banks("score_ps", 3), banks("o_ps", 2), banks("unit_ps", 3)
        ff1_ps = [(score_ps[0], score_ps[1]), (score_ps[2], unit_ps[2])]

        x0_in, x_in, wq_in, wo_in, rope_in = sem("x0_in"), sem("x_in"), sem("wq_in"), sem("wo_in"), sem("rope_in")
        c_in, ffw_in, bias_in = sem("c_in"), sem("ffw_in"), sem("bias_in")
        consts_ready, ident_zero, ident_ready = sem("consts_ready"), sem("ident_zero"), sem("ident_ready")
        w_hi_ready, w_lo_ready = sem("w_hi_ready"), sem("w_lo_ready")
        silu_exp, silu_steps, silu_ready = sem("silu_exp"), sem("silu_steps"), sem("silu_ready")
        c_t_ps, c_t_ready, mod_ps, mod_raw, mod_steps = (
            sem("c_t_ps"), sem("c_t_ready"), sem("mod_ps"), sem("mod_raw"), sem("mod_steps"))
        signs_ready, sign_ps, signs_t_ready = sem("signs_ready"), sem("sign_ps"), sem("signs_t_ready")
        alpha_raw, alpha_ready = sem("alpha_raw"), sem("alpha_ready")

        unit_full = sem("unit_full")

        ln_stats, ln_aggr, ln_var, ln_rstd, ln_out = (
            sem("ln_stats"), sem("ln_aggr"), sem("ln_var"), sem("ln_rstd"), sem("ln_out"))
        h_ready, h_hi_ready, h_lo_ready = sem("h_ready"), sem("h_hi_ready"), sem("h_lo_ready")
        v_ready, rot_parts, rot_high, rot_ready = sem("v_ready"), sem("rot_parts"), sem("rot_high"), sem("rot_ready")
        k_hi_ready, k_lo_ready, q_ready = sem("k_hi_ready"), sem("k_lo_ready"), sem("q_ready")
        q_hi_in = [sem(f"q_hi_in{i}") for i in range(4)]
        ident_r_ready = sem("ident_r_ready")
        max_ready, max_t_ready = sem("max_ready"), sem("max_t_ready")
        max_in = [sem(f"max_in{i}") for i in range(2)]
        scores_full, probs_ready, pv_done = sem("scores_full"), sem("probs_ready"), sem("pv_done")
        recip_ready, norm_ready, ot_ps_full, ot_ready = sem("recip_ready"), sem("norm_ready"), sem("ot_ps_full"), sem("ot_ready")
        z_ready, x2_ready = sem("z_ready"), sem("x2_ready")
        mlp_xt_full, mlp_h_ready, mlp_h_hi_ready, mlp_h_lo_ready = (
            sem("mlp_xt_full"), sem("mlp_h_ready"), sem("mlp_h_hi_ready"), sem("mlp_h_lo_ready"))
        ff1_done, gelu_done, ff2_done, mlp_z_ready, mlp_zt_full, y_ready = (
            sem("ff1_done"), sem("gelu_done"), sem("ff2_done"), sem("mlp_z_ready"), sem("mlp_zt_full"), sem("y_ready"))
        y_out = [sem(f"y_out{i}") for i in range(2)]

        block = ctx.enter_context(nc.Block())

        @block.sync
        def _(sp):
            sp.dma_start(xa[:, 0, :, :], x[0].rearrange("(c p) d -> p c d", p=P)).then_inc(x0_in, 16)
            sp.dma_start(c_sb[:, :], c).then_inc(c_in, 16)
            sp.dma_start(wmod_sb[:, :], wmod).then_inc(c_in, 16)
            sp.dma_start(w_all[:, 0:INNER], wq).then_inc(wq_in, 16)
            sp.dma_start(w_all[:, INNER:WIDE], wkv).then_inc(wq_in, 16)
            sp.dma_start(cos_sb[:, :, :], cos.rearrange("(c p) d -> p c d", p=P)).then_inc(rope_in, 16)
            sp.dma_start(sin_sb[:, :, :], sin.rearrange("(c p) d -> p c d", p=P)).then_inc(rope_in, 16)
            sp.dma_start(bo_sb[:, :], bo.rearrange("(p o) -> p o", o=1)).then_inc(bias_in, 16)
            sp.dma_start(b2_sb[:, :], b2.rearrange("(p o) -> p o", o=1)).then_inc(bias_in, 16)
            for k in range(KF):
                sp.dma_start(b1_sb[:, k:k + 1], b1[k * P:(k + 1) * P].rearrange("(p o) -> p o", o=1)).then_inc(bias_in, 16)
            for b in range(1, B, 5):
                sp.dma_start(xa[:, b:b + 5, :, :], x[b:b + 5].rearrange("b (c p) d -> p b c d", p=P)).then_inc(x_in, 16)
            sp.dma_start(wo_sb[:, :, :], wo.rearrange("(s p) n -> p s n", p=P)).then_inc(wo_in, 16)
            sp.dma_start(w1_sb[:, :, :], w1.rearrange("(k p) d -> p k d", p=P)).then_inc(ffw_in, 16)
            sp.dma_start(w2_sb[:, :], w2).then_inc(ffw_in, 16)

            def step(st):
                if not st.prep:
                    return

                def high_parts(quarter):
                    hs = slice(4 * quarter, 4 * quarter + 4)
                    sp.wait_ge(q_ready, st.count(8, 2 * quarter + 2, 1))
                    sp.dma_start(q_him[st.par(1)][0:DH, hs, :].bitcast(F32),
                                 q_hilo[st.par(1)][0:DH, hs, :].bitcast(F32)).then_inc(q_hi_in[quarter], 16)

                high_parts(0)
                high_parts(1)
                for half in range(2):
                    if half == 1:
                        high_parts(2)
                        high_parts(3)
                    sp.wait_ge(max_t_ready, st.count(2, half + 1, 1))
                    sp.dma_start(q_him[st.par(1)][DH:DH + 1, half * 8:half * 8 + 8, :].bitcast(F32)
                                 .rearrange("o h (c i) -> o (h c) i", c=C),
                                 neg_max_t[half][:, :].bitcast(F32)).then_inc(max_in[half], 16)

            attention_steps(sp, step)

            with sp.Fori(0, B // 2) as t:
                for odd in range(2):
                    sp.wait_ge(y_ready, t * 2 + (odd + 1))
                    sp.dma_start(out[bass.ds(t * 2 + odd, 1)].rearrange("b (c p) d -> p (b c) d", p=P),
                                 y_sb[odd][:, :, :]).then_inc(y_out[odd], 16)
            for odd in range(2):
                sp.wait_ge(y_out[odd], 16 * (B // 2))

        @block.gpsimd
        def _(pool):
            pool.memset(ident[:, :], 0.0).then_inc(ident_zero, 1)
            pool.memset(minus_half[:, :], -0.5).then_inc(consts_ready, 1)
            pool.wait_ge(ident_zero, 1)
            pool.affine_select(out=ident[:, :], in_=ident[:, :], compare_op=ALU.not_equal, fill=1.0,
                               base=0, pattern=[[-1, P]], channel_multiplier=1).then_inc(ident_ready, 1)
            for i in range(2):
                pool.memset(v_sb[i][:, :, :, DH:DH + 1], 1.0).then_inc(consts_ready, 1)

            def rsqrt(done):
                pool.wait_ge(ln_var, done)
                pool.tensor_tensor(rstd[:, :], var_eps[:, :], minus_half[:, :], ALU.pow).then_inc(ln_rstd, 1)

            pool.wait_ge(consts_ready, 5)

            def step(st):
                if not st.prep:
                    return
                rsqrt(st.count(1, 1, 1))
                for k, (ch, n) in enumerate(QKV_ORDER):
                    heads = 4 if n == 2 else 8
                    a, b = rot_a[k % 2][:, 0:heads, :], rot_b[k % 2][:, 0:heads, :]
                    high, low = (qk_rot[:, ch, 8 * n:8 * n + heads, i, :] for i in range(2))
                    pool.wait_ge(rot_parts, st.count(6, k + 1, 1))
                    if st.number != -1 or k > 0:
                        pool.wait_ge(rot_ready, st.count(6, k, 1))
                    pool.tensor_tensor(rot_sum[:, 0:heads, :], a, b, ALU.add)
                    pool.tensor_tensor(high, a, b, ALU.add).then_inc(rot_high, 1)
                    pool.wait_ge(rot_high, st.count(6, k + 1, 1))
                    pool.tensor_tensor(low, rot_sum[:, 0:heads, :], high.bitcast(F32), ALU.subtract).then_inc(rot_ready, 1)

            attention_steps(pool, step)
            with pool.Fori(0, B // 2) as t:
                rsqrt(t * 2 + (B + 1))
                rsqrt(t * 2 + (B + 2))

        @block.scalar
        def _(act):
            act.wait_ge(c_in, 32)
            act.activation(c_exp[:, :], c_sb[:, :], ACT.Exp, scale=-1.0).then_inc(silu_exp, 1)
            act.wait_ge(wq_in, 32)
            act.activation(w_hi[:, :], w_all[:, :], ACT.Copy).then_inc(w_hi_ready, 1)
            act.wait_ge(c_t_ps, 1)
            act.activation(c_t[:, :], o_ps[0][:, 0:B], ACT.Copy).then_inc(c_t_ready, 1)
            act.wait_ge(mod_steps, 8)

            act.wait_ge(ident_ready, 1)
            act.activation(ident_r[:, :], ident[:, :], ACT.Copy).then_inc(ident_r_ready, 1)

            def unit(st, place, u):
                kind, ps, par = u[0], unit_ps[UNIT_BANK[place]], st.par(1)
                if kind in ("s", "zT") or (kind == "qkv" and u[2] != 2):
                    return
                act.wait_ge(unit_full, nth_unit(st, place))
                if kind == "xT":
                    b = st.batch(1)
                    act.activation(h_t[:, :], ps[:, 0:N], ACT.Identity, scale=mod[:, 1, bass.ds(b, 1)],
                                   bias=mod[:, 0, bass.ds(b, 1)]).then_inc(h_ready, 1)
                    act.wait_ge(h_ready, st.count(1, 1, 1))
                    act.activation(h_hi[0][:, :], h_t[:, :], ACT.Copy).then_inc(h_hi_ready, 1)
                if kind == "qkv":
                    act.activation(v_sb[par][:, u[1], :, 0:DH],
                                   ps[:, 256:512].rearrange("p (g d) -> p g d", g=KV), ACT.Copy).then_inc(v_ready, 1)
                if kind == "kt":
                    high = ps[0:DH, :].rearrange("p (g i) -> p g i", g=2)
                    for half in range(2):
                        act.activation(k_hi2[par][half * DH:half * DH + DH, 2 * u[1]:2 * u[1] + 2, :], high,
                                       ACT.Copy).then_inc(k_hi_ready, 1)
                if kind == "qt":
                    act.activation(q_hilo[par][:, 2 * u[1]:2 * u[1] + 2, :],
                                   ps[:, :].rearrange("p (h i) -> p h i", h=2), ACT.Copy).then_inc(q_ready, 1)
                if kind == "mT":
                    if st.number != -1:
                        act.wait_ge(max_in[u[1]], st.count(16, 0, 1))
                    act.activation(neg_max_t[u[1]][:, :], ps[0:HEADS, 0:P], ACT.Copy).then_inc(max_t_ready, 1)
                if kind == "yT":
                    b = st.batch(-1)
                    act.activation(z_sb[:, :], ps[:, 0:N], ACT.Identity, scale=mod[:, 2, bass.ds(b, 1)],
                                   bias=ga_bo[:, bass.ds(b, 1)]).then_inc(z_ready, 1)

            def step(st):
                for s in range(PAIRS):
                    for place, w in slot_order(st, s):
                        if place is not None:
                            unit(st, place, w)
                        elif w[0] == "scores":
                            jc = w[1]
                            act.wait_ge(scores_full, st.count(16, 2 * s + jc + 1))
                            act.activation(probs[s % 2][:, jc, :, :].rearrange("p h i -> p (h i)"),
                                           score_ps[SCORE_BANK[2 * s + jc]][:, :], ACT.Exp, scale=SCALE).then_inc(probs_ready, 1)
                        elif w[0] == "ot":
                            act.wait_ge(ot_ps_full, st.count(8, s - 1))
                            act.activation(o_t[st.par(0 if s >= 2 else -1)][:, (s - 2) % 8, :], o_ps[s % 2][:, 0:N],
                                           ACT.Copy).then_inc(ot_ready, 1)

            attention_steps(act, step)

            act.wait_ge(ffw_in, 32)
            act.activation(sign1[:, :, :], w1_sb[:, :, :], ACT.Sign).then_inc(signs_ready, 1)
            act.activation(sign2[:, :], w2_sb[:, :], ACT.Sign).then_inc(signs_ready, 1)
            act.wait_ge(sign_ps, 1)
            act.activation(s1t[:, :, :], score_ps[0][:, :].rearrange("p (k f) -> p k f", k=KF), ACT.Copy).then_inc(signs_t_ready, 1)
            act.activation(s2t[:, :, :], score_ps[1][:, :].rearrange("p (k f) -> p k f", k=KF), ACT.Copy).then_inc(signs_t_ready, 1)
            act.wait_ge(alpha_ready, 1)

            def mlp_step(st):
                if st.mod:
                    b = st.batch(1)
                    act.wait_ge(mlp_xt_full, st.count(1, 1, 1))
                    if st.number != -1:
                        act.wait_ge(mlp_h_lo_ready, st.count(1, 0, 1))
                    act.activation(h_t[:, :], unit_ps[0][:, 0:N], ACT.Identity, scale=mod[:, 4, bass.ds(b, 1)],
                                   bias=mod[:, 3, bass.ds(b, 1)]).then_inc(mlp_h_ready, 1)
                    act.wait_ge(mlp_h_ready, st.count(1, 1, 1))
                    act.activation(h_hi[st.par(1)][:, :], h_t[:, :], ACT.Copy).then_inc(mlp_h_hi_ready, 1)
                if st.store:
                    b, par = st.batch(-2), st.par(0)
                    act.wait_ge(ff2_done, st.count(1, 1, -2))
                    act.activation(z_sb[:, :], o_ps[par][:, 0:N], ACT.Identity, scale=gb_alpha[:, bass.ds(b, 1)],
                                   bias=gb_b2[:, bass.ds(b, 1)]).then_inc(mlp_z_ready, 1)
                if st.ff1:
                    act.wait_ge(ff1_done, st.count(1, 1))
                    for k in range(KF):
                        act.activation(g_sb[st.par(0)][:, k, :], ff1_ps[st.par(0)][k // 2][:, (k % 2) * N:(k % 2) * N + N],
                                       ACT.Gelu, scale=alpha1[:, k:k + 1], bias=b1_sb[:, k:k + 1]).then_inc(gelu_done, 1)

            mlp_steps(act, mlp_step)

        @block.vector
        def _(dve):
            def layer_norm(done, b):
                for ch in range(C):
                    ins = dve.bn_stats(stats[:, ch, :], xa[:, bass.ds(b, 1), ch, :].rearrange("p b d -> p (b d)"))
                ins.then_inc(ln_stats, 1)
                dve.wait_ge(ln_stats, done)
                dve.memset(pause[:, :], 0.0)
                for ch in range(C):
                    ins = dve.bn_aggr(mean_var[:, ch, :], stats[:, ch, :])
                ins.then_inc(ln_aggr, 1)
                dve.wait_ge(ln_aggr, done)
                dve.tensor_scalar(var_eps[:, :], mean_var[:, :, 1], EPS, None, ALU.add).then_inc(ln_var, 1)
                dve.wait_ge(ln_rstd, done)
                for ch in range(C):
                    ins = dve.tensor_scalar(xn[:, ch, :], xa[:, bass.ds(b, 1), ch, :].rearrange("p b d -> p (b d)"),
                                            mean_var[:, ch, 0:1], rstd[:, ch:ch + 1], ALU.subtract, ALU.mult)
                ins.then_inc(ln_out, 1)

            for i in range(2):
                dve.memset(k_lo1[i][DH:DH + 1, :, :].bitcast(F32), 1.0).then_inc(consts_ready, 1)
            dve.wait_ge(silu_exp, 1)
            dve.tensor_scalar(c_exp[:, :], c_exp[:, :], 1.0, None, ALU.add).then_inc(silu_steps, 1)
            dve.wait_ge(silu_steps, 1)
            dve.reciprocal(c_exp[:, :], c_exp[:, :]).then_inc(silu_steps, 1)
            dve.wait_ge(silu_steps, 2)
            dve.tensor_tensor(c_silu[:, :], c_sb[:, :], c_exp[:, :], ALU.mult).then_inc(silu_ready, 1)
            dve.wait_ge(w_hi_ready, 1)
            dve.tensor_tensor(w_lo[:, :], w_all[:, :], w_hi[:, :].bitcast(F32), ALU.subtract).then_inc(w_lo_ready, 1)
            dve.wait_ge(mod_ps, 1)
            dve.tensor_copy(mod[:, :, :], o_ps[1][:, 0:6 * B].rearrange("p (k b) -> p k b", k=6)).then_inc(mod_raw, 1)
            dve.wait_ge(mod_raw, 1)
            for k in (1, 4):
                dve.tensor_scalar(mod[:, k, :], mod[:, k, :], 1.0, None, ALU.add)
            dve.wait_ge(bias_in, 16 * (2 + KF))
            for n, k in enumerate((2, 5)):
                dve.tensor_scalar(gate_sign[:, :], mod[:, k, :], 0.0, 2.0, ALU.is_ge, ALU.mult)
                dve.scalar_tensor_tensor(gate_abs[:, :], mod[:, k, :], -1.0, mod[:, k, :], ALU.mult,
                                         ALU.max).then_inc(mod_steps, 1)
                dve.wait_ge(mod_steps, 4 * n + 1)
                dve.tensor_scalar(gate_abs[:, :], gate_abs[:, :], 0.25, None, ALU.max).then_inc(mod_steps, 1)
                dve.wait_ge(mod_steps, 4 * n + 2)
                dve.scalar_tensor_tensor(mod[:, k, :], gate_sign[:, :], -1.0, gate_abs[:, :], ALU.add,
                                         ALU.mult).then_inc(mod_steps, 1)
                dve.wait_ge(mod_steps, 4 * n + 3)
                bias, into = ((bo_sb, ga_bo), (b2_sb, gb_b2))[n]
                dve.tensor_scalar(into[:, :], mod[:, k, :], bias[:, 0:1], None, ALU.mult).then_inc(mod_steps, 1)

            def unit(st, place, u):
                kind, ps, par = u[0], unit_ps[UNIT_BANK[place]], st.par(1)
                if kind in ("qt", "mT", "yT"):
                    return
                dve.wait_ge(unit_full, nth_unit(st, place))
                if kind == "xT":
                    dve.wait_ge(h_hi_ready, st.count(1, 1, 1))
                    dve.tensor_tensor(h_lo[0][:, :], h_t[:, :], h_hi[0][:, :].bitcast(F32), ALU.subtract).then_inc(h_lo_ready, 1)
                if kind == "qkv":
                    ch, n = u[1:]
                    k, heads = QKV_ORDER.index((ch, n)), 4 if n == 2 else 8
                    if n == 2:
                        dve.wait_ge(v_ready, st.count(2, ch + 1, 1))
                    if st.number != -1 or k >= 2:
                        dve.wait_ge(rot_ready, st.count(6, k - 1, 1))
                    raw = ps[:, 0:heads * DH].rearrange("p (h d) -> p h d", h=heads)
                    halves = ps[:, 0:heads * DH].rearrange("p (h t d) -> p h t d", h=heads, t=2)
                    dve.tensor_tensor(rot_a[k % 2][:, 0:heads, :], raw,
                                      cos_sb[:, ch:ch + 1, :].broadcast_to([P, heads, DH]), ALU.mult)
                    dve.tensor_tensor(rot_b[k % 2][:, 0:heads, :].rearrange("p h (t d) -> p h t d", t=2),
                                      halves[:, :, ::-1, :],
                                      sin_sb[:, ch:ch + 1, :].broadcast_to([P, heads, DH])
                                      .rearrange("p h (t d) -> p h t d", t=2), ALU.mult).then_inc(rot_parts, 1)
                if kind == "kt":
                    dve.wait_ge(k_hi_ready, st.count(4, 2 * u[1] + 2, 1))
                    dve.tensor_copy(k_lo1[par][0:DH, 2 * u[1]:2 * u[1] + 2, :],
                                    ps[DH:P, :].rearrange("p (g i) -> p g i", g=2)).then_inc(k_lo_ready, 1)
                if kind == "s":
                    dve.tensor_reduce(neg_max[:, u[1], :], ps[:, :].rearrange("p (c j) -> p c j", c=C), AX.X, ALU.max,
                                      negate=True).then_inc(max_ready, 1)
                if kind == "zT":
                    b = st.batch(-1)
                    dve.tensor_tensor(xa[:, bass.ds(b, 1), :, :].rearrange("p b c d -> p (b c) d"),
                                      ps[:, 0:N].rearrange("p (c d) -> p c d", c=C),
                                      xa[:, bass.ds(b, 1), :, :].rearrange("p b c d -> p (b c) d"),
                                      ALU.add).then_inc(x2_ready, 1)

            def normalise(st, s):
                i = s % 2
                groups = o_ps[i][:, 0:4 * (DH + 1)].rearrange("p (k e) -> p k e", e=DH + 1)
                dve.wait_ge(pv_done, st.count(8, s - 1))
                dve.reciprocal(recip[i][:, :].unsqueeze(2), groups[:, :, DH:DH + 1]).then_inc(recip_ready, 1)
                dve.wait_ge(recip_ready, st.count(8, s - 1))
                dve.tensor_tensor(o_norm[i][:, :, :, :].rearrange("p c h d -> p h c d"),
                                  groups[:, :, 0:DH].rearrange("p (h c) d -> p h c d", h=2),
                                  recip[i][:, :].rearrange("p (h c) -> p h c", h=2).unsqueeze(3)
                                  .broadcast_to([P, 2, C, DH]), ALU.mult).then_inc(norm_ready, 1)

            def step(st):
                if st.prep:
                    if st.number == -1:
                        dve.wait_ge(x0_in, 16)
                    layer_norm(st.count(1, 1, 1), st.batch(1))
                for s in range(PAIRS):
                    for place, w in slot_order(st, s):
                        if place is not None:
                            unit(st, place, w)
                        elif w[0] == "norm":
                            normalise(st, s)
                if st.number == -1:
                    dve.wait_ge(x_in, 48)

            dve.wait_ge(rope_in, 32)
            attention_steps(dve, step)

            dve.wait_ge(ffw_in, 32)
            dve.tensor_reduce(alpha1[:, :], w1_sb[:, :, :], AX.X, ALU.add, apply_absolute_value=True)
            dve.tensor_reduce(alpha2[:, :], w2_sb[:, :], AX.X, ALU.add, apply_absolute_value=True).then_inc(alpha_raw, 1)
            dve.wait_ge(alpha_raw, 1)
            dve.tensor_scalar(alpha1[:, :], alpha1[:, :], 1.0 / D, None, ALU.mult)
            dve.tensor_scalar(gb_alpha[:, :], mod[:, 5, :], alpha2[:, 0:1], 1.0 / FF, ALU.mult, ALU.mult).then_inc(alpha_ready, 1)

            def mlp_step(st):
                if st.mod:
                    dve.wait_ge(mlp_h_hi_ready, st.count(1, 1, 1))
                    dve.tensor_tensor(h_lo[st.par(1)][:, :], h_t[:, :], h_hi[st.par(1)][:, :].bitcast(F32),
                                      ALU.subtract).then_inc(mlp_h_lo_ready, 1)
                if st.norm:
                    if st.number != -2:
                        dve.wait_ge(mlp_xt_full, st.count(1, 0, 2))
                    layer_norm(st.count(1, B + 1, 2), st.batch(2))
                if st.store:
                    b, par = st.batch(-2), st.par(0)
                    dve.wait_ge(mlp_zt_full, st.count(1, 1, -2))
                    if st.number not in (2, 3):
                        dve.wait_ge(y_out[par], st.t * 16 + -16)
                    dve.tensor_tensor(y_sb[par][:, :, :], unit_ps[1][:, 0:N].rearrange("p (c d) -> p c d", c=C),
                                      xa[:, bass.ds(b, 1), :, :].rearrange("p b c d -> p (b c) d"),
                                      ALU.add).then_inc(y_ready, 1)

            mlp_steps(dve, mlp_step)

        @block.tensor
        def _(pe):
            pe.wait_ge(ident_ready, 1)
            pe.wait_ge(silu_ready, 1)
            pe.transpose(o_ps[0][:, 0:B], c_silu[:, :], ident[0:B, 0:B]).then_inc(c_t_ps, 1)
            pe.wait_ge(c_t_ready, 1)
            for k in range(6):
                ins = pe.matmul(o_ps[1][:, k * B:(k + 1) * B], wmod_sb[:, k * D:(k + 1) * D], c_t[:, :], start=True, stop=True)
            ins.then_inc(mod_ps, 1)

            pe.wait_ge(ident_r_ready, 1)

            def wait_for_reader(st, u, back):
                kind, ahead, behind = u[0], 1 - back, -1 - back
                if kind == "xT":
                    pe.wait_ge(h_ready, st.count(1, 1, ahead))
                if kind == "qkv":
                    pe.wait_ge(rot_parts, st.count(6, QKV_ORDER.index(u[1:]) + 1, ahead))
                if kind == "kt":
                    pe.wait_ge(k_lo_ready, st.count(2, u[1] + 1, ahead))
                if kind == "qt":
                    pe.wait_ge(q_ready, st.count(8, u[1] + 1, ahead))
                if kind == "s":
                    pe.wait_ge(max_ready, st.count(16, u[1] + 1, ahead))
                if kind == "mT":
                    pe.wait_ge(max_t_ready, st.count(2, u[1] + 1, ahead))
                if kind == "yT":
                    pe.wait_ge(z_ready, st.count(1, 1, behind))
                if kind == "zT":
                    pe.wait_ge(x2_ready, st.count(1, 1, behind))

            def unit(st, place, u):
                kind, ps, par = u[0], unit_ps[UNIT_BANK[place]], st.par(1)
                before = last_in_bank(st, place)
                if before:
                    wait_for_reader(st, *before)
                if kind == "xT":
                    pe.wait_ge(ln_out, st.count(1, 1, 1))
                    for ch in range(C):
                        ins = pe.transpose(ps[:, ch * P:(ch + 1) * P], xn[:, ch, :], ident[:, :])
                if kind == "qkv":
                    ch, n = u[1:]
                    if (ch, n) == QKV_ORDER[0]:
                        pe.wait_ge(h_lo_ready, st.count(1, 1, 1))
                        if st.number == -1:
                            pe.wait_ge(w_lo_ready, 1)
                    own, cols = slice(ch * P, (ch + 1) * P), slice(n * 512, (n + 1) * 512)
                    pe.matmul(ps[:, :], h_hi[0][:, own], w_hi[:, cols], start=True, stop=False)
                    pe.matmul(ps[:, :], h_hi[0][:, own], w_lo[:, cols], start=False, stop=False)
                    ins = pe.matmul(ps[:, :], h_lo[0][:, own], w_hi[:, cols], start=False, stop=True)
                if kind in ("kt", "qt"):
                    first = 2 * u[1] + (HEADS if kind == "kt" else 0)
                    if (kind, u[1]) == ("kt", 0):
                        pe.wait_ge(rot_ready, st.count(6, 2, 1))
                    if (kind, u[1]) == ("qt", 0):
                        pe.wait_ge(rot_ready, st.count(6, 4, 1))
                    if (kind, u[1]) == ("qt", 4):
                        pe.wait_ge(rot_ready, st.count(6, 6, 1))
                    for h in range(2):
                        for ch in range(C):
                            ins = pe.matmul(ps[:, h * N + ch * P:h * N + (ch + 1) * P],
                                            qk_rot[:, ch, first + h, :, :].rearrange("p t d -> p (t d)"),
                                            ident_r[:, :], start=True, stop=True)
                if kind == "s":
                    h, g = u[1], u[1] // GROUP
                    if h % 2 == 0:
                        pe.wait_ge(q_ready, st.count(8, h // 2 + 1, 1))
                    if h % 8 == 0:
                        pe.wait_ge(k_hi_ready, st.count(4, h // 4 + 2, 1))
                    for ch in range(C):
                        ins = pe.matmul(ps[:, ch * N:(ch + 1) * N], q_hilo[par][0:DH, h, ch * P:(ch + 1) * P],
                                        k_hi2[par][0:DH, g, :], start=True, stop=True)
                if kind == "mT":
                    pe.wait_ge(max_ready, st.count(16, 8 * (u[1] + 1), 1))
                    ins = pe.transpose(ps[0:HEADS, 0:P], neg_max[:, 8 * u[1]:8 * u[1] + 8, :].rearrange("p h c -> p (h c)"),
                                       ident[:, :])
                if kind == "yT":
                    pe.wait_ge(ot_ready, st.count(8, 0))
                    for s in range(PAIRS):
                        ins = pe.matmul(ps[:, 0:N], wo_sb[:, s, :], o_t[st.par(-1)][:, s, :], start=s == 0, stop=s == PAIRS - 1)
                if kind == "zT":
                    pe.wait_ge(z_ready, st.count(1, 1, -1))
                    for ch in range(C):
                        ins = pe.transpose(ps[:, ch * P:(ch + 1) * P], z_sb[:, ch * P:(ch + 1) * P], ident[:, :])
                ins.then_inc(unit_full, 1)

            def scores(st, s, jc):
                par, g, k = st.par(0), 2 * s // GROUP, 2 * s + jc
                if s % 4 == 0 and jc == 0:
                    pe.wait_ge(k_lo_ready, st.count(2, s // 4 + 1))
                    pe.wait_ge(max_in[s // 4], st.count(16, 16))
                if s % 2 == 0 and jc == 0:
                    pe.wait_ge(q_hi_in[s // 2], st.count(16, 16))
                last = max(j for j in range(k - 2 * PAIRS, k) if SCORE_BANK[j % (2 * PAIRS)] == SCORE_BANK[k])
                if st.number != 0 or last >= 0:
                    pe.wait_ge(probs_ready, st.count(16, last + 1))
                js, hs, ps = slice(jc * P, (jc + 1) * P), slice(2 * s, 2 * s + 2), score_ps[SCORE_BANK[k]]
                pe.matmul(ps[:, :], k_hi2[par][:, g, js],
                          q_hilo[par][:, hs, :].rearrange("p h i -> p (h i)"), start=True, stop=False)
                pe.matmul(ps[:, :], k_lo1[par][:, g, js], q_him[par][:, hs, :].rearrange("p h i -> p (h i)"),
                          start=False, stop=True).then_inc(scores_full, 1)

            def product_with_v(st, s, part):
                pair, par = (s - 1) % 8, st.par(0 if s >= 1 else -1)
                i, g, h, ch = pair % 2, 2 * pair // GROUP, part // C, part % C
                if part == 0:
                    pe.wait_ge(probs_ready, st.count(16, 2 * s))
                    if st.number != 0 or s >= 3:
                        pe.wait_ge(ot_ready, st.count(8, s - 2))
                into = o_ps[i][:, part * (DH + 1):(part + 1) * (DH + 1)]
                for jc in range(C):
                    ins = pe.matmul(into, probs[i][:, jc, h, ch * P:(ch + 1) * P], v_sb[par][:, jc, g, :],
                                    start=jc == 0, stop=jc == C - 1)
                if part == 3:
                    ins.then_inc(pv_done, 1)

            def step(st):
                if st.number == 0:
                    pe.wait_ge(consts_ready, 5)
                    pe.wait_ge(wo_in, 16)
                for s in range(PAIRS):
                    for place, w in slot_order(st, s):
                        if place is not None:
                            unit(st, place, w)
                        elif w[0] == "scores":
                            scores(st, s, w[1])
                        elif w[0] == "pv":
                            product_with_v(st, s, w[1])
                        elif w[0] == "ot":
                            i = s % 2
                            pe.wait_ge(norm_ready, st.count(8, s - 1))
                            for ch in range(C):
                                ins = pe.transpose(o_ps[i][:, ch * P:(ch + 1) * P],
                                                   o_norm[i][:, ch, :, :].rearrange("p h d -> p (h d)"), ident[:, :])
                            ins.then_inc(ot_ps_full, 1)

            attention_steps(pe, step)

            def mlp_step(st):
                if st.ff1:
                    pe.wait_ge(mlp_h_lo_ready, st.count(1, 1))
                    if st.number not in (0, 1):
                        pe.wait_ge(gelu_done, st.count(KF, 0, -1))
                    for k in range(KF):
                        into = ff1_ps[st.par(0)][k // 2][:, (k % 2) * N:(k % 2) * N + N]
                        pe.matmul(into, s1t[:, k, :], h_hi[st.par(0)][:, :], start=True, stop=False)
                        ins = pe.matmul(into, s1t[:, k, :], h_lo[st.par(0)][:, :], start=False, stop=True)
                    ins.then_inc(ff1_done, 1)
                if st.store:
                    pe.wait_ge(mlp_z_ready, st.count(1, 1, -2))
                    if st.number != 2:
                        pe.wait_ge(y_ready, st.count(1, 0, -2))
                    for ch in range(C):
                        ins = pe.transpose(unit_ps[1][:, ch * P:(ch + 1) * P], z_sb[:, ch * P:(ch + 1) * P], ident[:, :])
                    ins.then_inc(mlp_zt_full, 1)
                if st.ff2:
                    pe.wait_ge(gelu_done, st.count(KF, 0))
                    if st.number not in (1, 2):
                        pe.wait_ge(mlp_z_ready, st.count(1, 0, -2))
                    for k in range(KF):
                        ins = pe.matmul(o_ps[st.par(-1)][:, 0:N], s2t[:, k, :], g_sb[st.par(-1)][:, k, :],
                                        start=k == 0, stop=k == KF - 1)
                    ins.then_inc(ff2_done, 1)
                if st.norm:
                    pe.wait_ge(ln_out, st.count(1, B + 1, 2))
                    if st.number != -2:
                        pe.wait_ge(mlp_h_ready, st.count(1, 0, 2))
                    for ch in range(C):
                        ins = pe.transpose(unit_ps[0][:, ch * P:(ch + 1) * P], xn[:, ch, :], ident[:, :])
                    ins.then_inc(mlp_xt_full, 1)

            pe.wait_ge(signs_ready, 2)
            pe.wait_ge(probs_ready, 2 * B * PAIRS)
            pe.wait_ge(ot_ready, B * PAIRS)
            pe.wait_ge(z_ready, B)
            pe.wait_ge(x2_ready, B)
            for k in range(KF):
                pe.transpose(score_ps[0][:, k * P:(k + 1) * P], sign1[:, k, :], ident[:, :])
            for k in range(KF):
                ins = pe.transpose(score_ps[1][:, k * P:(k + 1) * P], sign2[:, k * P:(k + 1) * P], ident[:, :])
            ins.then_inc(sign_ps, 1)
            pe.wait_ge(signs_t_ready, 2)
            mlp_steps(pe, mlp_step)


_ORDER = ["L0_attn_x", "L0_attn_Wq", "L0_attn_Wkv", "L0_attn_Wo", "L0_attn_bo", "L0_ffn_w1", "L0_ffn_b1",
          "L0_ffn_w2", "L0_ffn_b2", "L0_c", "L0_wmod"]


def rotary_tables():
    inv_freq = (1.0 / 10000.0 ** (np.arange(0, DH, 2, dtype=np.float32) / np.float32(DH))).astype(np.float32)
    freqs = np.arange(N, dtype=np.float32)[:, None] * inv_freq[None, :]
    cos, sin = np.cos(freqs), np.sin(freqs)
    return (np.concatenate([cos, cos], 1).astype(np.float32), np.concatenate([-sin, sin], 1).astype(np.float32))


def kernel(**inputs):
    import concourse.bacc as bacc
    from concourse.bass_utils import run_bass_kernel_spmd

    nc = bacc.Bacc("TRN2", target_bir_lowering=False, num_devices=1)
    cos, sin = rotary_tables()
    arrays = {f"in_{name}": np.ascontiguousarray(inputs[name]) for name in _ORDER}
    arrays["in_cos"], arrays["in_sin"] = cos, sin
    args = [nc.dram_tensor(name, a.shape, F32, kind="ExternalInput").ap() for name, a in arrays.items()]
    out = nc.dram_tensor("out_x", (B, N, D), F32, kind="ExternalOutput").ap()
    adaln_layer(nc, *args, out)
    r = run_bass_kernel_spmd(nc, [arrays], core_ids=[0])
    return r.results[0]["out_x"]
```

```python
from contextlib import ExitStack

import numpy as np

import concourse.bass as bass
from concourse import mybir

F32 = mybir.dt.float32
F32R = mybir.dt.float32r
ALU = mybir.AluOpType
ACT = mybir.ActivationFunctionType
AX = mybir.AxisListType

P = 128
B, N, D = 16, 256, 128
C = N // P
HEADS, KV, DH = 16, 4, 64
GROUP = HEADS // KV
INNER = HEADS * DH
PAIRS = HEADS // 2
QK = HEADS + KV
WIDE = (HEADS + 2 * KV) * DH
FF = 512
KF = FF // P
SCALE = DH ** -0.5
EPS = 1e-5

UNITS = [
    [("s", 4), ("s", 5), ("s", 6), ("s", 7), ("xT", 0), ("qt", 4), ("mT", 1)],
    [("qkv", 0, 2), ("s", 8), ("qkv", 1, 2), ("qt", 5), ("s", 9)],
    [("s", 10), ("s", 11), ("qkv", 0, 0), ("qt", 6), ("mT", 2)],
    [("s", 12), ("qkv", 1, 0), ("bc", 4), ("bc", 5), ("kt", 0), ("qt", 7)],
    [("bc", 6), ("bc", 7), ("s", 13), ("s", 14), ("s", 15), ("yT", 0), ("mT", 3)],
    [("yT", 1), ("kt", 1), ("qkv", 0, 1), ("qt", 0), ("qt", 1)],
    [("s", 0), ("s", 1), ("s", 2), ("s", 3), ("qkv", 1, 1), ("mT", 0), ("zT", 0)],
    [("bc", 0), ("bc", 1), ("bc", 2), ("qt", 2), ("qt", 3), ("bc", 3)],
]
ALL_UNITS = [(slot, u) for slot, units in enumerate(UNITS) for u in units]
LATE_UNITS = ([("qt", s) for s in range(4, PAIRS)] + [("s", h) for h in range(4, HEADS)] + [("mT", q) for q in range(1, 4)]
              + [("bc", s) for s in range(4)])
OUT_UNITS = [("bc", s) for s in range(4, PAIRS)] + [("yT", 0), ("yT", 1), ("zT", 0)]
QKV_ORDER = [(0, 2), (1, 2), (0, 0), (1, 0), (0, 1), (1, 1)]


def unit_banks():
    banks, turn = [], 0
    for _, u in ALL_UNITS:
        if u == ("yT", 1):
            banks.append(first_half)
            assert turn - first_turn < 4
            continue
        if u == ("yT", 0):
            first_half, first_turn = turn % 4, turn
        banks.append(turn % 4)
        turn += 1
    return banks


UNIT_BANK = unit_banks()
TAIL_BANK = {u: (u[1] % 2 if u[0] == "bc" else int(u[0] == "zT")) for u in OUT_UNITS}
STATISTICS_AT, NORMALISE_AT, RECIPROCALS_AT = 4, 6, (5, 2)
SIGNS_AT = 4
ON_POOL = (1, 3, 4, 5, 7)
WORK = [("un",), ("scores", 0), ("scores", 1), ("pv", 0), ("pv", 1), ("pv", 2), ("pv", 3)]


class Step:

    def __init__(self, t, odd, **holds):
        self.t, self.odd, self.holds = t, odd, holds
        self.number = 2 * t + odd if isinstance(t, int) else None

    def __getattr__(self, name):
        return self.holds.get(name, False)

    def count(self, per, more, batch=0):
        return self.t * (2 * per) + (per * (self.odd + batch) + more)

    def batch(self, ahead):
        return self.t * 2 + (self.odd + ahead)

    def par(self, ahead):
        return (self.odd + ahead) % 2


def attention_steps(eng, body):
    body(Step(-1, 1, prep=True, norm=True))
    body(Step(0, 0, attn=True, prep=True, norm=True))
    with eng.Fori(0, B // 2 - 2) as t:
        body(Step(t, 1, attn=True, prep=True, out=True, norm=True))
        body(Step(t, 2, attn=True, prep=True, out=True, norm=True))
    body(Step(B // 2 - 2, 1, attn=True, prep=True, out=True, norm=True))
    body(Step(B // 2 - 2, 2, attn=True, prep=True, out=True, norm=True))
    body(Step(B // 2 - 1, 1, attn=True, out=True))
    body(Step(B // 2, 0, out=True, tail=True))


def mlp_steps(eng, body, first=False):
    def mlp_step(t, odd):
        n = 2 * t + odd
        body(Step(t, odd, norm=n < B - 2, mod=-1 <= n < B - 1, ff1=0 <= n < B, ff2=1 <= n <= B, store=n >= 2))

    if first:
        mlp_step(-1, 0)
        mlp_step(-1, 1)
        mlp_step(0, 0)
        return
    for n in range(1, 4):
        mlp_step(n // 2, n % 2)
    with eng.Fori(2, B // 2 - 1) as t:
        for odd in range(2):
            body(Step(t, odd, norm=True, mod=True, ff1=True, ff2=True, store=True))
    for n in range(B - 2, B + 2):
        mlp_step(n // 2, n % 2)


def has(st, u):
    return st.out if u in OUT_UNITS else st.attn if u in LATE_UNITS else st.prep


def ahead(u):
    return -1 if u in OUT_UNITS else 0 if u in LATE_UNITS else 1


def units(st, slot):
    return [(k, u) for k, (s, u) in enumerate(ALL_UNITS) if s == slot and has(st, u)]


def slot_order(st, s):
    held = {"scores": st.attn, "pv": st.attn if s >= 1 else st.out, "un": st.attn if s >= 2 else st.out}
    rest, order = units(st, s), []
    for w in WORK:
        if held[w[0]]:
            order.append((None, w))
            if rest and w[0] in ("scores", "pv"):
                order.append(rest.pop(0))
    return order + rest


def rotated(st, s, end):
    if end == st.attn or (st.attn and s == 0):
        return []
    return [u[1:] for _, u in units(st, s if end else s - 1) if u[0] == "qkv"]


def nth_unit(st, place):
    mine = sum(has(st, u) for _, u in ALL_UNITS[:place + 1])
    every, late, out = len(ALL_UNITS), len(LATE_UNITS), len(OUT_UNITS)
    first = every - out - late
    if st.number == -1:
        return mine
    if st.number == 0:
        return first + mine
    if st.tail:
        return first + (every - out) + (B - 2) * every + late + out + mine
    return st.count(every, first + (every - out) - every + mine)


def bank(st, place):
    return TAIL_BANK[ALL_UNITS[place][1]] if st.tail else UNIT_BANK[place]


def last_in_bank(st, place):
    for k in range(place - 1, -1, -1):
        if has(st, ALL_UNITS[k][1]) and bank(st, k) == bank(st, place):
            return ALL_UNITS[k][1], 0
    if st.number == -1:
        return None
    before = Step(0, 0, prep=not st.tail, attn=st.number != 0, out=st.number != 0)
    for k in range(len(ALL_UNITS) - 1, -1, -1):
        if UNIT_BANK[k] == bank(st, place) and has(before, ALL_UNITS[k][1]):
            assert st.tail or ALL_UNITS[k][1] not in OUT_UNITS
            return ALL_UNITS[k][1], 1


def adaln_layer(nc, x, wq, wkv, wo, bo, w1, b1, w2, b2, c, wmod, cos, sin, out):
    ctx = ExitStack()
    with ctx:
        def sb(name, shape, dt=F32):
            return ctx.enter_context(nc.sbuf_tensor(name, shape, dt))

        def sem(name):
            return ctx.enter_context(nc.semaphore(name))

        ident = sb("ident", [P, P])
        ident_r = sb("ident_r", [P, P], F32R)
        minus_half = sb("minus_half", [P, C])
        xa = sb("xa", [P, B, C, D])
        w_all = sb("w_all", [P, WIDE])
        w_hi = sb("w_hi", [P, WIDE], F32R)
        w_lo = sb("w_lo", [P, WIDE], F32R)
        wo_sb = sb("wo_sb", [P, PAIRS, D])
        cos_sb = sb("cos_sb", [P, C, DH])
        sin_sb = sb("sin_sb", [P, C, DH])
        w1_sb = sb("w1_sb", [P, KF, D])
        w2_sb = sb("w2_sb", [P, FF])
        alpha1 = sb("alpha1", [P, KF])
        alpha2 = sb("alpha2", [P, 1])
        b1_sb = sb("b1_sb", [P, KF])
        b2_sb = sb("b2_sb", [P, 1])
        bo_sb = sb("bo_sb", [P, 1])
        c_sb = sb("c_sb", [B, D])
        c_silu = sb("c_silu", [B, D])
        c_t = sb("c_t", [P, B])
        wmod_sb = sb("wmod_sb", [P, 6 * D])
        mod = sb("mod", [P, 6, B])
        gate_sign = sb("gate_sign", [P, B])
        gate_abs = sb("gate_abs", [P, B])
        ga_bo = sb("ga_bo", [P, B])
        gb_alpha = sb("gb_alpha", [P, B])
        gb_b2 = sb("gb_b2", [P, B])

        stats = sb("stats", [P, C, 6])
        pause = sb("pause", [P, 1])
        mean_var = sb("mean_var", [P, C, 2])
        var_eps = sb("var_eps", [P, C])
        rstd = sb("rstd", [P, C])
        xn = sb("xn", [P, C, D])
        h_t = sb("h_t", [P, N])
        h_hi = [sb(f"h_hi{i}", [P, N], F32R) for i in range(2)]
        h_lo = [sb(f"h_lo{i}", [P, N], F32R) for i in range(2)]
        rot_a = [sb(f"rot_a{i}", [P, 8, DH]) for i in range(2)]
        rot_b = [sb(f"rot_b{i}", [P, 8, DH]) for i in range(2)]
        rot_sum = [sb(f"rot_sum{i}", [P, 8, DH]) for i in range(2)]
        qk_rot = sb("qk_rot", [P, C, QK, 2, DH], F32R)
        v_hi = [sb(f"v_hi{i}", [P, C, KV, DH + 1], F32R) for i in range(2)]
        v_lo = [sb(f"v_lo{i}", [P, C, KV, DH + 1], F32R) for i in range(2)]
        k_hi2 = [sb(f"k_hi2{i}", [P, KV, N], F32R) for i in range(2)]
        k_lo1 = [sb(f"k_lo1{i}", [DH + 1, KV, N], F32R) for i in range(2)]
        q_hilo = [sb(f"q_hilo{i}", [P, HEADS, N], F32R) for i in range(2)]
        q_him = [sb(f"q_him{i}", [DH + 1, 4, N], F32R) for i in range(2)]
        neg_max = sb("neg_max", [P, HEADS, C])
        neg_max_t = [sb(f"neg_max_t{i}", [4 * C, P], F32R) for i in range(2)]
        probs = [sb(f"probs{i}", [P, C, 2, N]) for i in range(2)]
        probs_hi = [sb(f"probs_hi{i}", [P, C, 2, N], F32R) for i in range(2)]
        probs_lo = [sb(f"probs_lo{i}", [P, C, 2, N], F32R) for i in range(2)]
        o_un = sb("o_un", [DH + 1, PAIRS, 2, N])
        sums = sb("sums", [P, 16])
        recip = sb("recip", [P, 16])
        recip_hi = sb("recip_hi", [P, 16], F32R)
        recip_lo = sb("recip_lo", [P, 16], F32R)
        recip_parts = [sb(f"recip_parts{i}", [40, N], F32R) for i in range(2)]
        select = sb("select", [64, PAIRS, DH], F32R)
        o_t = sb("o_t", [P, PAIRS, N])
        z_sb = sb("z_sb", [P, N])
        s1t = sb("s1t", [P, KF, P], F32R)
        sign1 = probs[0][:, 0, :, :].rearrange("p h (k d) -> p (h k) d", k=2)
        sign2 = probs[0][:, 1, :, :].rearrange("p h i -> p (h i)")
        s2t = w_all[:, 0:FF].rearrange("p (k f) -> p k f", k=KF)
        g_sb, g_hi, g_lo = ([part[i][:, :, :, :].rearrange("p c h i -> p (c h) i") for i in range(2)]
                            for part in (probs, probs_hi, probs_lo))
        s2r = q_hilo[0][:, 0:2, :].rearrange("p a (b d) -> p (a b) d", b=2)
        y_sb = [w_all[:, FF + i * C * D:FF + (i + 1) * C * D].rearrange("p (c d) -> p c d", c=C) for i in range(2)]

        def banks(name, n):
            return [ctx.enter_context(nc.psum_tensor(f"{name}{i}", [P, 512], F32)) for i in range(n)]

        score_ps, o_ps, unit_ps = banks("score_ps", 2), banks("o_ps", 2), banks("unit_ps", 4)
        mlp_xt_ps, mlp_zt_ps, ff1_ps = score_ps[0], score_ps[1], [unit_ps[2:4], unit_ps[0:2]]

        x0_in, x_in, wq_in, wo_in, rope_in = sem("x0_in"), sem("x_in"), sem("wq_in"), sem("wo_in"), sem("rope_in")
        c_in, wmod_in, ffw_in, bias_in = sem("c_in"), sem("wmod_in"), sem("ffw_in"), sem("bias_in")
        consts_ready, ident_zero, ident_ready = sem("consts_ready"), sem("ident_zero"), sem("ident_ready")
        w_hi_ready, w_lo_ready = sem("w_hi_ready"), sem("w_lo_ready")
        silu_exp, silu_steps, silu_ready = sem("silu_exp"), sem("silu_steps"), sem("silu_ready")
        c_t_ps, c_t_ready, mod_ps, mod_raw, mod_shifts, mod_steps = (
            sem("c_t_ps"), sem("c_t_ready"), sem("mod_ps"), sem("mod_raw"), sem("mod_shifts"), sem("mod_steps"))
        signs_ready, sign_ps, signs_t_ready = sem("signs_ready"), sem("sign_ps"), sem("signs_t_ready")
        alpha_raw, alpha_ready = sem("alpha_raw"), sem("alpha_ready")

        unit_full = sem("unit_full")

        ln_stats, ln_aggr, ln_var, ln_rstd, ln_out = (
            sem("ln_stats"), sem("ln_aggr"), sem("ln_var"), sem("ln_rstd"), sem("ln_out"))
        h_ready, h_hi_ready, h_lo_ready = sem("h_ready"), sem("h_hi_ready"), sem("h_lo_ready")
        v_hi_ready, rot_parts, rot_summed, rot_high, rot_ready = (
            sem("v_hi_ready"), sem("rot_parts"), sem("rot_summed"), sem("rot_high"), sem("rot_ready"))
        k_hi_ready, k_lo_ready, q_ready = sem("k_hi_ready"), sem("k_lo_ready"), sem("q_ready")
        q_him_in = [sem(f"q_him_in{i}") for i in range(4)]
        ident_r_ready, select_ready = sem("ident_r_ready"), sem("select_ready")
        max_ready, max_t_ready = sem("max_ready"), sem("max_t_ready")
        scores_full, probs_ready, pv_done = sem("scores_full"), sem("probs_ready"), sem("pv_done")
        pool_lo_ready, dve_lo_ready = sem("pool_lo_ready"), sem("dve_lo_ready")
        o_un_ready, recip_ready, recip_hi_ready, recip_lo_ready, o_t_ready = (
            sem("o_un_ready"), sem("recip_ready"), sem("recip_hi_ready"), sem("recip_lo_ready"), sem("o_t_ready"))
        sums_in = [sem(f"sums_in{i}") for i in range(2)]
        recip_in = [sem(f"recip_in{i}") for i in range(2)]
        z_ready, x2_ready = sem("z_ready"), sem("x2_ready")
        mlp_xt_full, mlp_h_ready, mlp_h_hi_ready, mlp_h_lo_ready = (
            sem("mlp_xt_full"), sem("mlp_h_ready"), sem("mlp_h_hi_ready"), sem("mlp_h_lo_ready"))
        ff1_done, gelu_done, ff2_done, mlp_z_ready, mlp_zt_full, y_ready = (
            sem("ff1_done"), sem("gelu_done"), sem("ff2_done"), sem("mlp_z_ready"), sem("mlp_zt_full"), sem("y_ready"))
        s2r_ready, g_hi_ready, pool_g_lo_ready, dve_g_lo_ready = (
            sem("s2r_ready"), sem("g_hi_ready"), sem("pool_g_lo_ready"), sem("dve_g_lo_ready"))
        y_out = [sem(f"y_out{i}") for i in range(2)]

        block = ctx.enter_context(nc.Block())

        @block.sync
        def _(sp):
            sp.dma_start(c_sb[:, :], c).then_inc(c_in, 16)
            sp.dma_start(xa[:, 0, :, :], x[0].rearrange("(c p) d -> p c d", p=P)).then_inc(x0_in, 16)
            sp.dma_start(wmod_sb[:, :], wmod).then_inc(wmod_in, 16)
            sp.dma_start(w_all[:, 0:INNER], wq).then_inc(wq_in, 16)
            sp.dma_start(w_all[:, INNER:WIDE], wkv).then_inc(wq_in, 16)
            sp.dma_start(cos_sb[:, :, :], cos.rearrange("(c p) d -> p c d", p=P)).then_inc(rope_in, 16)
            sp.dma_start(sin_sb[:, :, :], sin.rearrange("(c p) d -> p c d", p=P)).then_inc(rope_in, 16)
            sp.dma_start(bo_sb[:, :], bo.rearrange("(p o) -> p o", o=1)).then_inc(bias_in, 16)
            sp.dma_start(b2_sb[:, :], b2.rearrange("(p o) -> p o", o=1)).then_inc(bias_in, 16)
            for k in range(KF):
                sp.dma_start(b1_sb[:, k:k + 1], b1[k * P:(k + 1) * P].rearrange("(p o) -> p o", o=1)).then_inc(bias_in, 16)
            sp.dma_start(w1_sb[:, :, :], w1.rearrange("(k p) d -> p k d", p=P)).then_inc(ffw_in, 16)
            sp.dma_start(w2_sb[:, :], w2).then_inc(ffw_in, 16)
            for b in range(1, B, 5):
                sp.dma_start(xa[:, b:b + 5, :, :], x[b:b + 5].rearrange("b (c p) d -> p b c d", p=P)).then_inc(x_in, 16)
            sp.dma_start(wo_sb[:, :, :], wo.rearrange("(s p) n -> p s n", p=P)).then_inc(wo_in, 16)

            def high_parts(st, quarter, batch):
                sp.wait_ge(q_ready, st.count(8, 2 * quarter + 2, batch))
                sp.dma_start(q_him[quarter % 2][0:DH, :, :].bitcast(F32),
                             q_hilo[st.par(batch)][0:DH, 4 * quarter:4 * quarter + 4, :].bitcast(F32)).then_inc(q_him_in[quarter], 16)

            def maxima(st, quarter, batch):
                sp.wait_ge(max_t_ready, st.count(4, quarter + 1, batch))
                sp.dma_start(q_him[quarter % 2][DH:DH + 1, :, :].bitcast(F32).rearrange("o h (c i) -> o (h c) i", c=C),
                             neg_max_t[quarter % 2][:, :].bitcast(F32)).then_inc(q_him_in[quarter], 16)

            def gather_sums(st, half, batch):
                sp.wait_ge(o_un_ready, st.count(8, 4 * half + 4, batch))
                sp.dma_start(sums[:, :], o_un[DH:DH + 1, 4 * half:4 * half + 4, :, :]
                             .rearrange("o s h (b t) -> o (s h b) t", t=16)).then_inc(sums_in[half], 16)

            def spread_reciprocals(st, half, batch):
                sp.wait_ge(recip_lo_ready, st.count(2, half + 1, batch))
                for first, part in ((0, recip_hi), (32, recip_lo)):
                    sp.dma_start(recip_parts[half][first:first + PAIRS, :].bitcast(F32).rearrange("h (b t) -> h b t", t=16),
                                 part[:, :].bitcast(F32)).then_inc(recip_in[half], 16)

            def step(st):
                if st.attn:
                    maxima(st, 1, 0)
                if st.out:
                    gather_sums(st, 1, -1)
                if st.attn:
                    high_parts(st, 2, 0)
                if st.out:
                    spread_reciprocals(st, 1, -1)
                if st.attn:
                    maxima(st, 2, 0)
                    high_parts(st, 3, 0)
                    maxima(st, 3, 0)
                    gather_sums(st, 0, 0)
                    spread_reciprocals(st, 0, 0)
                if st.prep:
                    high_parts(st, 0, 1)
                    maxima(st, 0, 1)
                    high_parts(st, 1, 1)

            attention_steps(sp, step)

            with sp.Fori(0, B // 2) as t:
                for odd in range(2):
                    sp.wait_ge(y_ready, t * 2 + (odd + 1))
                    sp.dma_start(out[bass.ds(t * 2 + odd, 1)].rearrange("b (c p) d -> p (b c) d", p=P),
                                 y_sb[odd][:, :, :]).then_inc(y_out[odd], 16)
            for odd in range(2):
                sp.wait_ge(y_out[odd], 16 * (B // 2))

        @block.gpsimd
        def _(pool):
            pool.memset(ident[:, :], 0.0).then_inc(ident_zero, 1)
            pool.memset(minus_half[:, :], -0.5).then_inc(consts_ready, 1)
            pool.wait_ge(ident_zero, 1)
            pool.affine_select(out=ident[:, :], in_=ident[:, :], compare_op=ALU.not_equal, fill=1.0,
                               base=0, pattern=[[-1, P]], channel_multiplier=1).then_inc(ident_ready, 1)
            for i in range(2):
                pool.memset(v_hi[i][:, :, :, DH:DH + 1].bitcast(F32), 1.0)
                pool.memset(v_lo[i][:, :, :, DH:DH + 1].bitcast(F32), 0.0).then_inc(consts_ready, 1)

            def rsqrt(done):
                pool.wait_ge(ln_var, done)
                pool.tensor_tensor(rstd[:, :], var_eps[:, :], minus_half[:, :], ALU.pow).then_inc(ln_rstd, 1)

            pool.wait_ge(consts_ready, 5)

            def rotation(st, ch, n, part):
                k, heads = QKV_ORDER.index((ch, n)), 4 if n == 2 else 8
                total = rot_sum[k % 2][:, 0:heads, :]
                high, low = (qk_rot[:, ch, 8 * n:8 * n + heads, i, :] for i in range(2))
                if part == 0:
                    pool.wait_ge(rot_parts, st.count(6, k + 1, 1))
                    if st.number != -1 or k >= 2:
                        pool.wait_ge(rot_ready, st.count(6, k - 1, 1))
                    pool.tensor_tensor(total, rot_a[k % 2][:, 0:heads, :], rot_b[k % 2][:, 0:heads, :],
                                       ALU.add).then_inc(rot_summed, 1)
                if part == 1:
                    pool.wait_ge(rot_high, st.count(6, k + 1, 1))
                    pool.tensor_tensor(low, total, high.bitcast(F32), ALU.subtract).then_inc(rot_ready, 1)

            def step(st):
                for s in range(PAIRS):
                    if st.norm and s == STATISTICS_AT + 1:
                        rsqrt(st.count(1, 1, 2))
                    for place, w in slot_order(st, s):
                        if w == ("scores", 1):
                            for jc in range(2 if s in ON_POOL else 1):
                                pool.wait_ge(probs_ready, st.count(16, 2 * s + jc + 1))
                                pool.tensor_tensor(probs_lo[s % 2][:, jc, :, :], probs[s % 2][:, jc, :, :],
                                                   probs_hi[s % 2][:, jc, :, :].bitcast(F32),
                                                   ALU.subtract).then_inc(pool_lo_ready, 1)
                        if w[0] == "qkv":
                            rotation(st, *w[1:], 0)
                            k = QKV_ORDER.index(w[1:])
                            if not st.attn and 1 <= k <= 3:
                                rotation(st, *QKV_ORDER[k - 1], 1)
                        if w == ("scores", 1):
                            for w in rotated(st, s, False):
                                rotation(st, *w, 1)
                    for w in rotated(st, s, True):
                        if QKV_ORDER.index(w) >= 3:
                            rotation(st, *w, 1)

            rsqrt(1)
            attention_steps(pool, step)

            def mlp_step(st):
                if st.norm and st.number != -2:
                    rsqrt(st.count(1, B + 1, 2))
                if st.ff2:
                    pool.wait_ge(g_hi_ready, st.count(1, 1, -1))
                    pool.tensor_tensor(g_lo[st.par(-1)][:, 0:3, :], g_sb[st.par(-1)][:, 0:3, :],
                                       g_hi[st.par(-1)][:, 0:3, :].bitcast(F32), ALU.subtract).then_inc(pool_g_lo_ready, 1)

            mlp_steps(pool, mlp_step, first=True)
            mlp_steps(pool, mlp_step)

        @block.scalar
        def _(act):
            act.wait_ge(c_in, 16)
            act.activation(c_silu[:, :], c_sb[:, :], ACT.Exp, scale=-1.0).then_inc(silu_exp, 1)
            act.wait_ge(wq_in, 32)
            act.activation(w_hi[:, :], w_all[:, :], ACT.Copy).then_inc(w_hi_ready, 1)
            act.wait_ge(c_t_ps, 1)
            act.activation(c_t[:, :], o_ps[0][:, 0:B], ACT.Copy).then_inc(c_t_ready, 1)
            act.wait_ge(mod_shifts, 1)

            act.wait_ge(ident_ready, 1)
            act.activation(ident_r[:, :], ident[:, :], ACT.Copy).then_inc(ident_r_ready, 1)

            def unit(st, place, u):
                kind, ps, par = u[0], unit_ps[bank(st, place)], st.par(ahead(u))
                if kind in ("s", "zT", "bc") or (kind == "qkv" and u[2] != 2) or u == ("yT", 0):
                    return
                act.wait_ge(unit_full, nth_unit(st, place))
                if kind == "xT":
                    b = st.batch(1)
                    act.activation(h_t[:, :], ps[:, 0:N], ACT.Identity, scale=mod[:, 1, bass.ds(b, 1)],
                                   bias=mod[:, 0, bass.ds(b, 1)]).then_inc(h_ready, 1)
                    act.wait_ge(h_ready, st.count(1, 1, 1))
                    act.activation(h_hi[0][:, :], h_t[:, :], ACT.Copy).then_inc(h_hi_ready, 1)
                if kind == "qkv":
                    act.activation(v_hi[par][:, u[1], :, 0:DH],
                                   ps[:, 256:512].rearrange("p (g d) -> p g d", g=KV), ACT.Copy).then_inc(v_hi_ready, 1)
                if kind == "kt":
                    high = ps[0:DH, :].rearrange("p (g i) -> p g i", g=2)
                    for half in range(2):
                        act.activation(k_hi2[par][half * DH:half * DH + DH, 2 * u[1]:2 * u[1] + 2, :], high,
                                       ACT.Copy).then_inc(k_hi_ready, 1)
                    act.activation(k_lo1[par][0:DH, 2 * u[1]:2 * u[1] + 2, :],
                                   ps[DH:P, :].rearrange("p (g i) -> p g i", g=2), ACT.Copy).then_inc(k_lo_ready, 1)
                if kind == "qt":
                    act.activation(q_hilo[par][:, 2 * u[1]:2 * u[1] + 2, :],
                                   ps[:, :].rearrange("p (h i) -> p h i", h=2), ACT.Copy).then_inc(q_ready, 1)
                if kind == "mT":
                    quarter = u[1]
                    if st.number != (-1, 0, None, None)[quarter]:
                        act.wait_ge(q_him_in[(quarter - 2) % 4], st.count(32, -32 if quarter < 2 else 0, ahead(u) + 1))
                    act.activation(neg_max_t[quarter % 2][:, :], ps[0:4 * C, 0:P], ACT.Copy).then_inc(max_t_ready, 1)
                if kind == "yT":
                    b = st.batch(-1)
                    act.activation(z_sb[:, :], ps[:, 0:N], ACT.Identity, scale=mod[:, 2, bass.ds(b, 1)],
                                   bias=ga_bo[:, bass.ds(b, 1)]).then_inc(z_ready, 1)

            def rotation_high(st, ch, n):
                k, heads = QKV_ORDER.index((ch, n)), 4 if n == 2 else 8
                act.wait_ge(rot_summed, st.count(6, k + 1, 1))
                act.activation(qk_rot[:, ch, 8 * n:8 * n + heads, 0, :], rot_sum[k % 2][:, 0:heads, :],
                               ACT.Copy).then_inc(rot_high, 1)

            def signs():
                for half in range(2):
                    act.activation(select[32 * half:32 * half + 32, :, :],
                                   ident[0:32, 0:PAIRS].unsqueeze(2).broadcast_to([32, PAIRS, DH]), ACT.Copy).then_inc(select_ready, 1)
                act.wait_ge(mod_steps, 8)
                act.wait_ge(ffw_in, 32)
                act.activation(sign1[:, :, :], w1_sb[:, :, :], ACT.Sign).then_inc(signs_ready, 1)
                act.activation(sign2[:, :], w2_sb[:, :], ACT.Sign).then_inc(signs_ready, 1)
                act.wait_ge(sign_ps, 1)
                act.activation(s1t[:, :, :], score_ps[0][:, :].rearrange("p (k f) -> p k f", k=KF), ACT.Copy).then_inc(signs_t_ready, 1)
                act.activation(s2t[:, :, :], score_ps[1][:, :].rearrange("p (k f) -> p k f", k=KF), ACT.Copy).then_inc(signs_t_ready, 1)

            def mlp_step(st):
                if st.number == -2:
                    act.activation(s2r[:, :, :], s2t[:, :, :], ACT.Copy).then_inc(s2r_ready, 1)
                if st.number == 0:
                    act.wait_ge(alpha_ready, 1)
                if st.mod:
                    b = st.batch(1)
                    act.wait_ge(mlp_xt_full, st.count(1, 1, 1))
                    if st.number != -1:
                        act.wait_ge(mlp_h_lo_ready, st.count(1, 0, 1))
                    act.activation(h_t[:, :], mlp_xt_ps[:, 0:N], ACT.Identity, scale=mod[:, 4, bass.ds(b, 1)],
                                   bias=mod[:, 3, bass.ds(b, 1)]).then_inc(mlp_h_ready, 1)
                if st.store:
                    b, par = st.batch(-2), st.par(0)
                    act.wait_ge(ff2_done, st.count(1, 1, -2))
                    act.activation(z_sb[:, :], o_ps[par][:, 0:N], ACT.Identity, scale=gb_alpha[:, bass.ds(b, 1)],
                                   bias=gb_b2[:, bass.ds(b, 1)]).then_inc(mlp_z_ready, 1)
                if st.ff1:
                    act.wait_ge(ff1_done, st.count(1, 1))
                    for k in range(KF):
                        act.activation(g_sb[st.par(0)][:, k, :], ff1_ps[st.par(0)][k // 2][:, (k % 2) * N:(k % 2) * N + N],
                                       ACT.Gelu, scale=alpha1[:, k:k + 1], bias=b1_sb[:, k:k + 1]).then_inc(gelu_done, 1)

            def step(st):
                for s in range(PAIRS):
                    for place, w in slot_order(st, s):
                        if place is not None:
                            unit(st, place, w)
                        elif w[0] == "scores":
                            jc = w[1]
                            act.wait_ge(scores_full, st.count(16, 2 * s + jc + 1))
                            act.activation(probs[s % 2][:, jc, :, :].rearrange("p h i -> p (h i)"),
                                           score_ps[jc][:, :], ACT.Exp, scale=SCALE)
                            act.activation(probs_hi[s % 2][:, jc, :, :].rearrange("p h i -> p (h i)"),
                                           score_ps[jc][:, :], ACT.Exp, scale=SCALE).then_inc(probs_ready, 1)
                        elif w[0] == "un":
                            act.wait_ge(pv_done, st.count(8, s - 1))
                            act.activation(o_un[:, (s - 2) % 8, :, :].rearrange("p h i -> p (h i)"), o_ps[s % 2][0:DH + 1, :],
                                           ACT.Copy).then_inc(o_un_ready, 1)
                        if w == ("scores", 1):
                            for w in rotated(st, s, False):
                                rotation_high(st, *w)
                    for w in rotated(st, s, True):
                        rotation_high(st, *w)
                    if st.number == -1 and s == SIGNS_AT:
                        signs()
                    if st.tail and s == 1:
                        mlp_steps(act, mlp_step, first=True)

            attention_steps(act, step)

            mlp_steps(act, mlp_step)

        @block.vector
        def _(dve):
            def row(b, ch):
                return xa[:, bass.ds(b, 1), ch, :].rearrange("p b d -> p (b d)")

            def statistics(done, b):
                for ch in range(C):
                    ins = dve.bn_stats(stats[:, ch, :], row(b, ch))
                ins.then_inc(ln_stats, 1)
                dve.wait_ge(ln_stats, done)
                dve.memset(pause[:, :], 0.0)
                for ch in range(C):
                    ins = dve.bn_aggr(mean_var[:, ch, :], stats[:, ch, :])
                ins.then_inc(ln_aggr, 1)
                dve.wait_ge(ln_aggr, done)
                dve.tensor_scalar(var_eps[:, :], mean_var[:, :, 1], EPS, None, ALU.add).then_inc(ln_var, 1)

            def normalise_tokens(done, b):
                dve.wait_ge(ln_rstd, done)
                for ch in range(C):
                    ins = dve.tensor_scalar(xn[:, ch, :], row(b, ch), mean_var[:, ch, 0:1], rstd[:, ch:ch + 1],
                                            ALU.subtract, ALU.mult)
                ins.then_inc(ln_out, 1)

            for i in range(2):
                dve.memset(recip_parts[i][:, :].bitcast(F32), 0.0)
                dve.memset(k_lo1[i][DH:DH + 1, :, :].bitcast(F32), 1.0).then_inc(consts_ready, 1)
            dve.wait_ge(x0_in, 16)
            statistics(1, 0)
            dve.wait_ge(silu_exp, 1)
            dve.tensor_scalar(c_silu[:, :], c_silu[:, :], 1.0, None, ALU.add).then_inc(silu_steps, 1)
            dve.wait_ge(silu_steps, 1)
            dve.reciprocal(c_silu[:, :], c_silu[:, :]).then_inc(silu_steps, 1)
            dve.wait_ge(silu_steps, 2)
            dve.tensor_tensor(c_silu[:, :], c_sb[:, :], c_silu[:, :], ALU.mult).then_inc(silu_ready, 1)
            normalise_tokens(1, 0)
            dve.wait_ge(w_hi_ready, 1)
            dve.tensor_tensor(w_lo[:, :], w_all[:, :], w_hi[:, :].bitcast(F32), ALU.subtract).then_inc(w_lo_ready, 1)
            dve.wait_ge(mod_ps, 1)
            dve.tensor_copy(mod[:, :, :], o_ps[1][:, 0:6 * B].rearrange("p (k b) -> p k b", k=6)).then_inc(mod_raw, 1)
            dve.wait_ge(mod_raw, 1)
            for k in (1, 4):
                ins = dve.tensor_scalar(mod[:, k, :], mod[:, k, :], 1.0, None, ALU.add)
            ins.then_inc(mod_shifts, 1)
            def unit(st, place, u):
                kind, ps, par = u[0], unit_ps[bank(st, place)], st.par(ahead(u))
                if kind in ("kt", "qt", "mT", "yT"):
                    return
                dve.wait_ge(unit_full, nth_unit(st, place))
                if kind == "xT":
                    dve.wait_ge(h_hi_ready, st.count(1, 1, 1))
                    dve.tensor_tensor(h_lo[0][:, :], h_t[:, :], h_hi[0][:, :].bitcast(F32), ALU.subtract).then_inc(h_lo_ready, 1)
                if kind == "qkv":
                    ch, n = u[1:]
                    k, heads = QKV_ORDER.index((ch, n)), 4 if n == 2 else 8
                    if n == 2:
                        dve.wait_ge(v_hi_ready, st.count(2, ch + 1, 1))
                        dve.tensor_tensor(v_lo[par][:, ch, :, 0:DH], ps[:, 256:512].rearrange("p (g d) -> p g d", g=KV),
                                          v_hi[par][:, ch, :, 0:DH].bitcast(F32), ALU.subtract)
                    if st.number != -1 or k >= 2:
                        dve.wait_ge(rot_summed, st.count(6, k - 1, 1))
                    raw = ps[:, 0:heads * DH].rearrange("p (h d) -> p h d", h=heads)
                    halves = ps[:, 0:heads * DH].rearrange("p (h t d) -> p h t d", h=heads, t=2)
                    dve.tensor_tensor(rot_a[k % 2][:, 0:heads, :], raw,
                                      cos_sb[:, ch:ch + 1, :].broadcast_to([P, heads, DH]), ALU.mult)
                    dve.tensor_tensor(rot_b[k % 2][:, 0:heads, :].rearrange("p h (t d) -> p h t d", t=2),
                                      halves[:, :, ::-1, :],
                                      sin_sb[:, ch:ch + 1, :].broadcast_to([P, heads, DH])
                                      .rearrange("p h (t d) -> p h t d", t=2), ALU.mult).then_inc(rot_parts, 1)
                if kind == "s":
                    dve.tensor_reduce(neg_max[:, u[1], :], ps[:, :].rearrange("p (c j) -> p c j", c=C), AX.X, ALU.max,
                                      negate=True).then_inc(max_ready, 1)
                if kind == "bc":
                    for h in range(2):
                        ins = dve.tensor_tensor(o_t[h * DH:h * DH + DH, u[1], :], o_un[0:DH, u[1], h, :],
                                                ps[h * DH:h * DH + DH, 0:N], ALU.mult)
                    ins.then_inc(o_t_ready, 1)
                if kind == "zT":
                    b = st.batch(-1)
                    dve.tensor_tensor(xa[:, bass.ds(b, 1), :, :].rearrange("p b c d -> p (b c) d"),
                                      ps[:, 0:N].rearrange("p (c d) -> p c d", c=C),
                                      xa[:, bass.ds(b, 1), :, :].rearrange("p b c d -> p (b c) d"),
                                      ALU.add).then_inc(x2_ready, 1)

            def reciprocals(st, half, batch):
                dve.wait_ge(sums_in[half], st.count(16, 16, batch))
                dve.reciprocal(recip[:, :], sums[:, :]).then_inc(recip_ready, 1)
                dve.wait_ge(recip_ready, st.count(2, half + 1, batch))
                dve.tensor_copy(recip_hi[:, :], recip[:, :]).then_inc(recip_hi_ready, 1)
                dve.wait_ge(recip_hi_ready, st.count(2, half + 1, batch))
                dve.tensor_tensor(recip_lo[:, :], recip[:, :], recip_hi[:, :].bitcast(F32),
                                  ALU.subtract).then_inc(recip_lo_ready, 1)

            def gates():
                dve.wait_ge(bias_in, 16 * (2 + KF))
                for n, k in enumerate((2, 5)):
                    dve.tensor_scalar(gate_sign[:, :], mod[:, k, :], 0.0, 2.0, ALU.is_ge, ALU.mult)
                    dve.scalar_tensor_tensor(gate_abs[:, :], mod[:, k, :], -1.0, mod[:, k, :], ALU.mult,
                                             ALU.max).then_inc(mod_steps, 1)
                    dve.wait_ge(mod_steps, 4 * n + 1)
                    dve.tensor_scalar(gate_abs[:, :], gate_abs[:, :], 0.25, None, ALU.max).then_inc(mod_steps, 1)
                    dve.wait_ge(mod_steps, 4 * n + 2)
                    dve.scalar_tensor_tensor(mod[:, k, :], gate_sign[:, :], -1.0, gate_abs[:, :], ALU.add,
                                             ALU.mult).then_inc(mod_steps, 1)
                    dve.wait_ge(mod_steps, 4 * n + 3)
                    bias, into = ((bo_sb, ga_bo), (b2_sb, gb_b2))[n]
                    dve.tensor_scalar(into[:, :], mod[:, k, :], bias[:, 0:1], None, ALU.mult).then_inc(mod_steps, 1)

            def alphas():
                dve.wait_ge(ffw_in, 32)
                dve.tensor_reduce(alpha1[:, :], w1_sb[:, :, :], AX.X, ALU.add, apply_absolute_value=True)
                dve.tensor_reduce(alpha2[:, :], w2_sb[:, :], AX.X, ALU.add, apply_absolute_value=True).then_inc(alpha_raw, 1)
                dve.wait_ge(alpha_raw, 1)
                dve.tensor_scalar(alpha1[:, :], alpha1[:, :], 1.0 / D, None, ALU.mult)
                dve.tensor_scalar(gb_alpha[:, :], mod[:, 5, :], alpha2[:, 0:1], 1.0 / FF, ALU.mult, ALU.mult).then_inc(alpha_ready, 1)

            def mlp_step(st):
                if st.norm and st.number != -2:
                    statistics(st.count(1, B + 1, 2), st.batch(2))
                if st.ff2:
                    dve.wait_ge(gelu_done, st.count(KF, 0))
                    dve.tensor_copy(g_hi[st.par(-1)][:, :, :], g_sb[st.par(-1)][:, :, :]).then_inc(g_hi_ready, 1)
                if st.mod:
                    dve.wait_ge(mlp_h_ready, st.count(1, 1, 1))
                    dve.tensor_copy(h_hi[st.par(1)][:, :], h_t[:, :]).then_inc(mlp_h_hi_ready, 1)
                    dve.wait_ge(mlp_h_hi_ready, st.count(1, 1, 1))
                    dve.tensor_tensor(h_lo[st.par(1)][:, :], h_t[:, :], h_hi[st.par(1)][:, :].bitcast(F32),
                                      ALU.subtract).then_inc(mlp_h_lo_ready, 1)
                if st.norm and st.number != -2:
                    dve.wait_ge(mlp_xt_full, st.count(1, 0, 2))
                    normalise_tokens(st.count(1, B + 1, 2), st.batch(2))
                if st.ff2:
                    dve.wait_ge(g_hi_ready, st.count(1, 1, -1))
                    dve.tensor_tensor(g_lo[st.par(-1)][:, 3, :], g_sb[st.par(-1)][:, 3, :],
                                      g_hi[st.par(-1)][:, 3, :].bitcast(F32), ALU.subtract).then_inc(dve_g_lo_ready, 1)
                if st.store:
                    b, par = st.batch(-2), st.par(0)
                    dve.wait_ge(mlp_zt_full, st.count(1, 1, -2))
                    if st.number not in (2, 3):
                        dve.wait_ge(y_out[par], st.t * 16 + -16)
                    dve.tensor_tensor(y_sb[par][:, :, :], mlp_zt_ps[:, 0:N].rearrange("p (c d) -> p c d", c=C),
                                      xa[:, bass.ds(b, 1), :, :].rearrange("p b c d -> p (b c) d"),
                                      ALU.add).then_inc(y_ready, 1)

            def step(st):
                for s in range(PAIRS):
                    if st.norm and s == STATISTICS_AT:
                        if st.number == -1:
                            dve.wait_ge(x_in, 48)
                        statistics(st.count(1, 1, 2), 0 if st.number == B - 2 else st.batch(2))
                    if st.norm and s == NORMALISE_AT:
                        normalise_tokens(st.count(1, 1, 2), 0 if st.number == B - 2 else st.batch(2))
                    if st.out and s == RECIPROCALS_AT[1]:
                        reciprocals(st, 1, -1)
                    if st.attn and s == RECIPROCALS_AT[0]:
                        reciprocals(st, 0, 0)
                    for place, w in slot_order(st, s):
                        if place is not None:
                            unit(st, place, w)
                    if st.attn and s not in ON_POOL:
                        dve.wait_ge(probs_ready, st.count(16, 2 * s + 2))
                        dve.tensor_tensor(probs_lo[s % 2][:, 1, :, :], probs[s % 2][:, 1, :, :],
                                          probs_hi[s % 2][:, 1, :, :].bitcast(F32), ALU.subtract).then_inc(dve_lo_ready, 1)
                    if st.number == -1 and s == SIGNS_AT:
                        gates()
                        alphas()
                    if st.tail and s == 1:
                        mlp_steps(dve, mlp_step, first=True)

            dve.wait_ge(rope_in, 32)
            attention_steps(dve, step)

            mlp_steps(dve, mlp_step)

        @block.tensor
        def _(pe):
            pe.wait_ge(ident_ready, 1)
            pe.wait_ge(silu_ready, 1)
            pe.transpose(o_ps[0][:, 0:B], c_silu[:, :], ident[0:B, 0:B]).then_inc(c_t_ps, 1)
            pe.wait_ge(c_t_ready, 1)
            pe.wait_ge(wmod_in, 16)
            for k in range(6):
                ins = pe.matmul(o_ps[1][:, k * B:(k + 1) * B], wmod_sb[:, k * D:(k + 1) * D], c_t[:, :], start=True, stop=True)
            ins.then_inc(mod_ps, 1)

            def wait_for_reader(st, u, back):
                kind, of = u[0], ahead(u) - back
                if kind == "xT":
                    pe.wait_ge(h_ready, st.count(1, 1, of))
                if kind == "qkv":
                    pe.wait_ge(rot_parts, st.count(6, QKV_ORDER.index(u[1:]) + 1, of))
                if kind == "kt":
                    pe.wait_ge(k_lo_ready, st.count(2, u[1] + 1, of))
                if kind == "qt":
                    pe.wait_ge(q_ready, st.count(8, u[1] + 1, of))
                if kind == "s":
                    pe.wait_ge(max_ready, st.count(16, u[1] + 1, of))
                if kind == "mT":
                    pe.wait_ge(max_t_ready, st.count(4, u[1] + 1, of))
                if kind == "bc":
                    pe.wait_ge(o_t_ready, st.count(8, u[1] + 1, of))
                if kind == "yT":
                    pe.wait_ge(z_ready, st.count(1, 1, of))
                if kind == "zT":
                    pe.wait_ge(x2_ready, st.count(1, 1, of))

            def unit(st, place, u):
                kind, ps, par = u[0], unit_ps[bank(st, place)], st.par(ahead(u))
                before = last_in_bank(st, place)
                if before and u != ("yT", 1):
                    wait_for_reader(st, *before)
                if kind == "xT":
                    pe.wait_ge(ln_out, st.count(1, 1, 1))
                    for ch in range(C):
                        ins = pe.transpose(ps[:, ch * P:(ch + 1) * P], xn[:, ch, :], ident[:, :])
                if kind == "qkv":
                    ch, n = u[1:]
                    if (ch, n) == QKV_ORDER[0]:
                        pe.wait_ge(h_lo_ready, st.count(1, 1, 1))
                        if st.number == -1:
                            pe.wait_ge(w_lo_ready, 1)
                    own, cols = slice(ch * P, (ch + 1) * P), slice(n * 512, (n + 1) * 512)
                    pe.matmul(ps[:, :], h_hi[0][:, own], w_hi[:, cols], start=True, stop=False)
                    pe.matmul(ps[:, :], h_hi[0][:, own], w_lo[:, cols], start=False, stop=False)
                    ins = pe.matmul(ps[:, :], h_lo[0][:, own], w_hi[:, cols], start=False, stop=True)
                if kind in ("kt", "qt"):
                    first = 2 * u[1] + (HEADS if kind == "kt" else 0)
                    if (st.number, kind, u[1]) == (-1, "kt", 0):
                        pe.wait_ge(ident_r_ready, 1)
                    if (kind, u[1]) == ("kt", 0):
                        pe.wait_ge(rot_ready, st.count(6, 2, 1))
                    if (kind, u[1]) == ("qt", 0):
                        pe.wait_ge(rot_ready, st.count(6, 4, 1))
                    if (kind, u[1]) == ("qt", 4):
                        pe.wait_ge(rot_ready, st.count(6, 6))
                    for h in range(2):
                        for ch in range(C):
                            ins = pe.matmul(ps[:, h * N + ch * P:h * N + (ch + 1) * P],
                                            qk_rot[:, ch, first + h, :, :].rearrange("p t d -> p (t d)"),
                                            ident_r[:, :], start=True, stop=True)
                if kind == "s":
                    h, g = u[1], u[1] // GROUP
                    if h % 2 == 0:
                        pe.wait_ge(q_ready, st.count(8, h // 2 + 1, ahead(u)))
                    if h % 8 == 0:
                        pe.wait_ge(k_hi_ready, st.count(4, h // 4 + 2, ahead(u)))
                    for ch in range(C):
                        ins = pe.matmul(ps[:, ch * N:(ch + 1) * N], q_hilo[par][0:DH, h, ch * P:(ch + 1) * P],
                                        k_hi2[par][0:DH, g, :], start=True, stop=True)
                if kind == "mT":
                    pe.wait_ge(max_ready, st.count(16, 4 * (u[1] + 1), ahead(u)))
                    ins = pe.transpose(ps[0:4 * C, 0:P], neg_max[:, 4 * u[1]:4 * u[1] + 4, :].rearrange("p h c -> p (h c)"),
                                       ident[:, :])
                if kind == "bc":
                    half = u[1] // 4
                    if u[1] % 4 == 0:
                        pe.wait_ge(recip_in[half], st.count(32, 32, ahead(u)))
                    ins = pe.matmul(ps[:, 0:N], select[0:40, 2 * (u[1] % 4):2 * (u[1] % 4) + 2, :].rearrange("k h d -> k (h d)"),
                                    recip_parts[half][:, :], start=True, stop=True)
                if kind == "yT":
                    pe.wait_ge(o_t_ready, st.count(8, 0))
                    own = slice(u[1] * P, (u[1] + 1) * P)
                    for s in range(PAIRS):
                        ins = pe.matmul(ps[:, own], wo_sb[:, s, :], o_t[:, s, own],
                                        start=s == 0, stop=s == PAIRS - 1)
                if kind == "zT":
                    pe.wait_ge(z_ready, st.count(1, 1, -1))
                    for ch in range(C):
                        ins = pe.transpose(ps[:, ch * P:(ch + 1) * P], z_sb[:, ch * P:(ch + 1) * P], ident[:, :])
                ins.then_inc(unit_full, 1)

            def scores(st, s, jc):
                par, g, k = st.par(0), 2 * s // GROUP, 2 * s + jc
                if s % 4 == 0 and jc == 0:
                    pe.wait_ge(k_lo_ready, st.count(2, s // 4 + 1))
                if s % 2 == 0 and jc == 0:
                    pe.wait_ge(q_him_in[s // 2], st.count(32, 32))
                if st.number != 0 or s > 0:
                    pe.wait_ge(probs_ready, st.count(16, k - 1))
                js, hs, ps = slice(jc * P, (jc + 1) * P), slice(2 * s, 2 * s + 2), score_ps[jc]
                pe.matmul(ps[:, :], k_hi2[par][:, g, js],
                          q_hilo[par][:, hs, :].rearrange("p h i -> p (h i)"), start=True, stop=False)
                pe.matmul(ps[:, :], k_lo1[par][:, g, js],
                          q_him[s // 2 % 2][:, s % 2 * 2:s % 2 * 2 + 2, :].rearrange("p h i -> p (h i)"),
                          start=False, stop=True).then_inc(scores_full, 1)

            def product_with_v(st, s, part):
                pair, par = (s - 1) % 8, st.par(0 if s >= 1 else -1)
                i, g = pair % 2, 2 * pair // GROUP
                if part == 0:
                    pe.wait_ge(probs_ready, st.count(16, 2 * s))
                    if st.number != 0 or s >= 3:
                        pe.wait_ge(o_un_ready, st.count(8, s - 2))
                if part >= 2:
                    on_pool, every = sum(q <= pair for q in ON_POOL), 8 + len(ON_POOL)
                    batch = 0 if s >= 1 else -1
                    if part == 3 and pair not in ON_POOL:
                        pe.wait_ge(dve_lo_ready, st.count(16 - every, pair + 1 - on_pool, batch))
                    else:
                        last_first = part == 2 and pair in ON_POOL
                        pe.wait_ge(pool_lo_ready, st.count(every, pair + 1 + on_pool - last_first, batch))
                p, v, chunks = [(probs_hi, v_hi, (0, 1)), (probs_hi, v_lo, (0, 1)),
                                (probs_lo, v_hi, (0,)), (probs_lo, v_hi, (1,))][part]
                for jc in chunks:
                    ins = pe.matmul(o_ps[i][0:DH + 1, :], v[par][:, jc, g, :], p[i][:, jc, :, :].rearrange("p h i -> p (h i)"),
                                    start=part == 0 and jc == 0, stop=part == 3)
                if part == 3:
                    ins.then_inc(pv_done, 1)

            def signs():
                pe.wait_ge(signs_ready, 2)
                for k in range(KF):
                    pe.transpose(score_ps[0][:, k * P:(k + 1) * P], sign1[:, k, :], ident[:, :])
                for k in range(KF):
                    ins = pe.transpose(score_ps[1][:, k * P:(k + 1) * P], sign2[:, k * P:(k + 1) * P], ident[:, :])
                ins.then_inc(sign_ps, 1)

            def mlp_step(st):
                if st.number == -2:
                    pe.wait_ge(probs_ready, 2 * B * PAIRS)
                if st.number == 0:
                    pe.wait_ge(q_ready, 8 * B)
                    pe.wait_ge(max_ready, 16 * B)
                    pe.wait_ge(max_t_ready, 4 * B)
                    pe.wait_ge(o_t_ready, 8 * B - 4)
                    pe.wait_ge(x2_ready, B - 1)
                if st.number == 1:
                    pe.wait_ge(x2_ready, B)
                    pe.wait_ge(o_un_ready, B * PAIRS)
                if st.ff1:
                    pe.wait_ge(mlp_h_lo_ready, st.count(1, 1))
                    if st.number not in (0, 1):
                        pe.wait_ge(gelu_done, st.count(KF, 0, -1))
                    for k in range(KF):
                        into = ff1_ps[st.par(0)][k // 2][:, (k % 2) * N:(k % 2) * N + N]
                        pe.matmul(into, s1t[:, k, :], h_hi[st.par(0)][:, :], start=True, stop=False)
                        ins = pe.matmul(into, s1t[:, k, :], h_lo[st.par(0)][:, :], start=False, stop=True)
                    ins.then_inc(ff1_done, 1)
                if st.store:
                    pe.wait_ge(mlp_z_ready, st.count(1, 1, -2))
                    if st.number != 2:
                        pe.wait_ge(y_ready, st.count(1, 0, -2))
                    for ch in range(C):
                        ins = pe.transpose(mlp_zt_ps[:, ch * P:(ch + 1) * P], z_sb[:, ch * P:(ch + 1) * P], ident[:, :])
                    ins.then_inc(mlp_zt_full, 1)
                if st.norm:
                    pe.wait_ge(ln_out, st.count(1, B + 1, 2))
                    if st.number != -2:
                        pe.wait_ge(mlp_h_ready, st.count(1, 0, 2))
                    for ch in range(C):
                        ins = pe.transpose(mlp_xt_ps[:, ch * P:(ch + 1) * P], xn[:, ch, :], ident[:, :])
                    ins.then_inc(mlp_xt_full, 1)
                if st.ff2:
                    if st.number == 1:
                        pe.wait_ge(s2r_ready, 1)
                    if st.number not in (1, 2):
                        pe.wait_ge(mlp_z_ready, st.count(1, 0, -2))
                    for part, g in enumerate((g_hi, g_lo)):
                        if part == 0:
                            pe.wait_ge(g_hi_ready, st.count(1, 1, -1))
                        else:
                            pe.wait_ge(pool_g_lo_ready, st.count(1, 1, -1))
                            pe.wait_ge(dve_g_lo_ready, st.count(1, 1, -1))
                        for k in range(KF):
                            ins = pe.matmul(o_ps[st.par(-1)][:, 0:N], s2r[:, k, :], g[st.par(-1)][:, k, :],
                                            start=(part, k) == (0, 0), stop=(part, k) == (1, KF - 1))
                    ins.then_inc(ff2_done, 1)

            def step(st):
                if st.number == 0:
                    pe.wait_ge(consts_ready, 5)
                    pe.wait_ge(select_ready, 2)
                    pe.wait_ge(wo_in, 16)
                    pe.wait_ge(signs_t_ready, 2)
                for s in range(PAIRS):
                    for place, w in slot_order(st, s):
                        if place is not None:
                            unit(st, place, w)
                        elif w[0] == "scores":
                            scores(st, s, w[1])
                        elif w[0] == "pv":
                            product_with_v(st, s, w[1])
                    if st.number == -1 and s == SIGNS_AT:
                        signs()
                    if st.tail and s == 1:
                        mlp_steps(pe, mlp_step, first=True)

            attention_steps(pe, step)

            mlp_steps(pe, mlp_step)


_ORDER = ["L0_attn_x", "L0_attn_Wq", "L0_attn_Wkv", "L0_attn_Wo", "L0_attn_bo", "L0_ffn_w1", "L0_ffn_b1",
          "L0_ffn_w2", "L0_ffn_b2", "L0_c", "L0_wmod"]


def rotary_tables():
    inv_freq = (1.0 / 10000.0 ** (np.arange(0, DH, 2, dtype=np.float32) / np.float32(DH))).astype(np.float32)
    freqs = np.arange(N, dtype=np.float32)[:, None] * inv_freq[None, :]
    cos, sin = np.cos(freqs), np.sin(freqs)
    return (np.concatenate([cos, cos], 1).astype(np.float32), np.concatenate([-sin, sin], 1).astype(np.float32))


def kernel(**inputs):
    import concourse.bacc as bacc
    from concourse.bass_utils import run_bass_kernel_spmd

    nc = bacc.Bacc("TRN2", target_bir_lowering=False, num_devices=1)
    cos, sin = rotary_tables()
    arrays = {f"in_{name}": np.ascontiguousarray(inputs[name]) for name in _ORDER}
    arrays["in_cos"], arrays["in_sin"] = cos, sin
    args = [nc.dram_tensor(name, a.shape, F32, kind="ExternalInput").ap() for name, a in arrays.items()]
    out = nc.dram_tensor("out_x", (B, N, D), F32, kind="ExternalOutput").ap()
    adaln_layer(nc, *args, out)
    r = run_bass_kernel_spmd(nc, [arrays], core_ids=[0])
    return r.results[0]["out_x"]
```
